# Optimizing a Trainium2 kernel written in Bass

```python
import numpy as np
import jax
import jax.numpy as jnp

def _softmax(x, axis=-1):
    return jax.nn.softmax(x, axis=axis)

def _gelu(x):
    return jax.nn.gelu(x, approximate=True)

def _silu(x):
    return jax.nn.silu(x)

def _sigmoid(x):
    return jax.nn.sigmoid(x)

def _layernorm(x, axis=-1, eps=1e-05):
    m = jnp.mean(x, axis=axis, keepdims=True)
    v = jnp.var(x, axis=axis, keepdims=True)
    return (x - m) / jnp.sqrt(v + eps)

def _scatter_add(tgt, idx, src, axis=0):
    return tgt.at[idx].add(src)

def _segment_sum(src, seg, n):
    return jax.ops.segment_sum(src, seg, n)
kernel_name = 'mk_vit_tower_cls_d1_tok_img1024_r4_01a92c'

def setup_inputs(seed: int=0):
    np.random.seed(seed)
    _w = jnp.asarray

    def _rec_inputs():
        import jax
        import jax.numpy as jnp
        _rk = jax.random.key(seed)
        x = -0.00016672 + 0.999947 * jax.random.normal(jax.random.fold_in(_rk, 1), (16, 96, 96, 3), jnp.float32)
        cls_tok = 0.02 * jax.random.normal(jax.random.fold_in(_rk, 5), (1, 1, 256), jnp.float32)
        return (x, cls_tok)
    x, cls_tok = _rec_inputs()

    def _L0_tok_setup():
        import jax, jax.numpy as jnp
        import numpy as np
        P = 16
        E = 256

        def patchify(images, patch_size):
            B, H, W, C = images.shape
            hp, wp = (H // patch_size, W // patch_size)
            x = images.reshape(B, hp, patch_size, wp, patch_size, C)
            x = x.transpose(0, 1, 3, 2, 4, 5)
            return x.reshape(B, hp * wp, patch_size * patch_size * C)
        key = jax.random.key(seed)
        k_img, k_w, k_b, k_pos = jax.random.split(key, 4)
        B, H, W, C = (64, 96, 96, 3)
        patch_dim = P * P * C
        patch_count = H // P * (W // P)
        images = jax.random.normal(k_img, (B, H, W, C), dtype=jnp.float32)
        W_proj = jax.random.normal(k_w, (E, patch_dim), dtype=jnp.float32) * patch_dim ** (-0.5)
        b_proj = jax.random.normal(k_b, (E,), dtype=jnp.float32) * 0.02
        pos_emb = jax.random.normal(k_pos, (patch_count, E), dtype=jnp.float32) * 0.02
        return {'images': images, 'W_proj': W_proj, 'b_proj': b_proj, 'pos_emb': pos_emb}
    _L0_tok_all = _L0_tok_setup()
    _L0_tok_in = {k: v for k, v in _L0_tok_all.items() if k in ('W_proj', 'b_proj', 'pos_emb')}
    del _L0_tok_all

    def _L0_attn_setup():
        import jax, jax.numpy as jnp
        import numpy as np
        B, S, D, H = (4, 512, 256, 4)
        HD = D // H

        def _reference_tuple_inner(hidden_states, Wq, Wk, Wv, Wo, bo, betas, mem, z):
            b, s, d = hidden_states.shape
            h = betas.shape[1]
            hd = d // h

            def split(x):
                return x.reshape(b, s, h, hd).transpose(0, 2, 1, 3)
            q = split(hidden_states @ Wq.T)
            k = split(hidden_states @ Wk.T)
            v = split(hidden_states @ Wv.T)
            aw = jnp.einsum('bhqd,bhkd->bhqk', q, k)
            causal = jnp.tril(jnp.ones((s, s), bool))
            aw = jnp.where(causal, aw, jnp.finfo(aw.dtype).min)
            p = jax.nn.softmax(aw, axis=-1)
            attn = jnp.einsum('bhqk,bhkd->bhqd', p, v)
            sq = jax.nn.elu(q) + 1.0
            sk = jax.nn.elu(k) + 1.0
            A_mem = jnp.einsum('bhsd,hde->bhse', sq, mem) / (jnp.einsum('bhsd,hdo->bhso', sq, z) + 1e-06)
            g = jax.nn.sigmoid(betas)
            out = g * A_mem + (1.0 - g) * attn
            delta = jnp.einsum('bhsd,hde->bhse', sk, mem) / (jnp.einsum('bhsd,hdo->bhso', sk, z) + 1e-06)
            mem_new = mem + jnp.einsum('bhsd,bhse->hde', sk, v - delta) / b
            z_new = z + jnp.mean(jnp.sum(sk, axis=2), axis=0)[:, :, None]
            out = out.transpose(0, 2, 1, 3).reshape(b, s, d)
            out = out @ Wo.T + bo
            return (out, mem_new, z_new)
        key = jax.random.key(seed)
        ks = jax.random.split(key, 6)
        s = 0.02
        return {'hidden_states': jax.random.normal(ks[0], (B, S, D), jnp.float32), 'Wq': jax.random.normal(ks[1], (D, D), jnp.float32) * s, 'Wk': jax.random.normal(ks[2], (D, D), jnp.float32) * s, 'Wv': jax.random.normal(ks[3], (D, D), jnp.float32) * s, 'Wo': jax.random.normal(ks[4], (D, D), jnp.float32) * s, 'bo': jnp.zeros((D,), jnp.float32), 'betas': jax.random.normal(ks[5], (1, H, 1, 1), jnp.float32), 'mem': jnp.zeros((H, HD, HD), jnp.float32), 'z': jnp.zeros((H, HD, 1), jnp.float32)}
    _L0_attn_all = _L0_attn_setup()
    _L0_attn_in = {k: v for k, v in _L0_attn_all.items() if k in ('Wq', 'Wk', 'Wv', 'Wo', 'bo', 'betas', 'mem', 'z')}
    del _L0_attn_all

    def _L0_ffn_setup():
        import math
        import jax, jax.numpy as jnp
        import numpy as np
        D_MODEL = 256
        D_FF = 1024
        E = 8
        K = 2
        CAP_FACTOR = 1.25
        CLAMP = 10000.0
        LN_EPS = 1e-05
        B, S = (2, 512)
        key = jax.random.key(seed)
        ks = jax.random.split(key, 6)
        b12 = math.sqrt(6.0 / (D_MODEL + 2 * D_FF))
        b3 = math.sqrt(6.0 / (D_FF + D_MODEL))
        br = 0.02 * math.sqrt(3.0)
        return {'x': jax.random.normal(ks[0], (B, S, D_MODEL), dtype=jnp.float32), 'ln_gamma': jnp.ones((D_MODEL,), jnp.float32), 'ln_beta': jnp.zeros((D_MODEL,), jnp.float32), 'router_w': jax.random.uniform(ks[1], (E, D_MODEL), jnp.float32, -br, br), 'w12': jax.random.uniform(ks[2], (E, 2 * D_FF, D_MODEL), jnp.float32, -b12, b12), 'w3': jax.random.uniform(ks[3], (E, D_MODEL, D_FF), jnp.float32, -b3, b3)}
    _L0_ffn_all = _L0_ffn_setup()
    _L0_ffn_in = {k: v for k, v in _L0_ffn_all.items() if k in ('ln_gamma', 'ln_beta', 'router_w', 'w12', 'w3')}
    del _L0_ffn_all
    return {'x': x, 'cls_tok': cls_tok, 'L0_tok_W_proj': _L0_tok_in['W_proj'], 'L0_tok_b_proj': _L0_tok_in['b_proj'], 'L0_tok_pos_emb': _L0_tok_in['pos_emb'], 'L0_attn_Wq': _L0_attn_in['Wq'], 'L0_attn_Wk': _L0_attn_in['Wk'], 'L0_attn_Wv': _L0_attn_in['Wv'], 'L0_attn_Wo': _L0_attn_in['Wo'], 'L0_attn_bo': _L0_attn_in['bo'], 'L0_attn_betas': _L0_attn_in['betas'], 'L0_attn_mem': _L0_attn_in['mem'], 'L0_attn_z': _L0_attn_in['z'], 'L0_ffn_ln_gamma': _L0_ffn_in['ln_gamma'], 'L0_ffn_ln_beta': _L0_ffn_in['ln_beta'], 'L0_ffn_router_w': _L0_ffn_in['router_w'], 'L0_ffn_w12': _L0_ffn_in['w12'], 'L0_ffn_w3': _L0_ffn_in['w3']}

def reference(x, cls_tok, L0_tok_W_proj, L0_tok_b_proj, L0_tok_pos_emb, L0_attn_Wq, L0_attn_Wk, L0_attn_Wv, L0_attn_Wo, L0_attn_bo, L0_attn_betas, L0_attn_mem, L0_attn_z, L0_ffn_ln_gamma, L0_ffn_ln_beta, L0_ffn_router_w, L0_ffn_w12, L0_ffn_w3):
    import jax
    import jax.numpy as jnp

    def _L0_tok_ref(images, W_proj, b_proj, pos_emb):
        import jax, jax.numpy as jnp
        import numpy as np
        P = 16
        E = 256

        def patchify(images, patch_size):
            B, H, W, C = images.shape
            hp, wp = (H // patch_size, W // patch_size)
            x = images.reshape(B, hp, patch_size, wp, patch_size, C)
            x = x.transpose(0, 1, 3, 2, 4, 5)
            return x.reshape(B, hp * wp, patch_size * patch_size * C)
        patches = patchify(images, P)
        out = jnp.einsum('bnd,ed->bne', patches, W_proj) + b_proj + pos_emb[None, :, :]
        return out

    def _L0_attn_ref(hidden_states, Wq, Wk, Wv, Wo, bo, betas, mem, z):
        import jax, jax.numpy as jnp
        import numpy as np
        B, S, D, H = (4, 512, 256, 4)
        HD = D // H

        def _reference_tuple_inner(hidden_states, Wq, Wk, Wv, Wo, bo, betas, mem, z):
            b, s, d = hidden_states.shape
            h = betas.shape[1]
            hd = d // h

            def split(x):
                return x.reshape(b, s, h, hd).transpose(0, 2, 1, 3)
            q = split(hidden_states @ Wq.T)
            k = split(hidden_states @ Wk.T)
            v = split(hidden_states @ Wv.T)
            aw = jnp.einsum('bhqd,bhkd->bhqk', q, k)
            causal = jnp.tril(jnp.ones((s, s), bool))
            aw = jnp.where(causal, aw, jnp.finfo(aw.dtype).min)
            p = jax.nn.softmax(aw, axis=-1)
            attn = jnp.einsum('bhqk,bhkd->bhqd', p, v)
            sq = jax.nn.elu(q) + 1.0
            sk = jax.nn.elu(k) + 1.0
            A_mem = jnp.einsum('bhsd,hde->bhse', sq, mem) / (jnp.einsum('bhsd,hdo->bhso', sq, z) + 1e-06)
            g = jax.nn.sigmoid(betas)
            out = g * A_mem + (1.0 - g) * attn
            delta = jnp.einsum('bhsd,hde->bhse', sk, mem) / (jnp.einsum('bhsd,hdo->bhso', sk, z) + 1e-06)
            mem_new = mem + jnp.einsum('bhsd,bhse->hde', sk, v - delta) / b
            z_new = z + jnp.mean(jnp.sum(sk, axis=2), axis=0)[:, :, None]
            out = out.transpose(0, 2, 1, 3).reshape(b, s, d)
            out = out @ Wo.T + bo
            return (out, mem_new, z_new)
        return _reference_tuple_inner(hidden_states, Wq, Wk, Wv, Wo, bo, betas, mem, z)[0]

    def _L0_ffn_ref(x, ln_gamma, ln_beta, router_w, w12, w3):
        import math
        import jax, jax.numpy as jnp
        import numpy as np
        D_MODEL = 256
        D_FF = 1024
        E = 8
        K = 2
        CAP_FACTOR = 1.25
        CLAMP = 10000.0
        LN_EPS = 1e-05
        B, S = (2, 512)
        Bq, Sq, D = x.shape
        T = Bq * Sq
        mu = jnp.mean(x, axis=-1, keepdims=True)
        var = jnp.mean(jnp.square(x - mu), axis=-1, keepdims=True)
        xn = (x - mu) * jax.lax.rsqrt(var + LN_EPS) * ln_gamma + ln_beta
        xf = xn.reshape(T, D)
        logits = jnp.clip(xf @ router_w.T, -CLAMP, CLAMP)
        top_v, top_i = jax.lax.top_k(logits, K)
        m = jnp.max(top_v, axis=-1, keepdims=True)
        ev = jnp.exp(top_v - m)
        top_p = ev / (jnp.sum(ev, axis=-1, keepdims=True) + 1e-12)
        Stot = T * K
        experts = top_i.reshape(-1)
        weights = top_p.reshape(-1)
        tokens = jnp.repeat(jnp.arange(T), K)
        oh = (experts[:, None] == jnp.arange(E)[None, :]).astype(jnp.int32)
        pos = jnp.take_along_axis(jnp.cumsum(oh, axis=0) - 1, experts[:, None], axis=1)[:, 0]
        C = max(1, math.ceil(T * K * CAP_FACTOR / E))
        kept = pos < C
        slot = jnp.where(kept, experts * C + pos, E * C)
        buf = jnp.zeros((E * C + 1, D), x.dtype).at[slot].set(xf[tokens])
        xb = buf[:E * C].reshape(E, C, D)
        gu = jnp.einsum('ecd,efd->ecf', xb, w12)
        g, u = jnp.split(gu, 2, axis=-1)
        h = jax.nn.silu(g) * u
        yb = jnp.einsum('ecf,edf->ecd', h, w3).reshape(E * C, D)
        ys = yb[jnp.minimum(slot, E * C - 1)] * (weights * kept.astype(weights.dtype))[:, None]
        out = jnp.zeros((T, D), x.dtype).at[tokens].add(ys)
        return out.reshape(Bq, Sq, D)
    h = _L0_tok_ref(x, L0_tok_W_proj, L0_tok_b_proj, L0_tok_pos_emb)
    h = jnp.concatenate([jnp.broadcast_to(cls_tok, (h.shape[0], 1, h.shape[2])), h], axis=1)
    h = h + _L0_attn_ref(_layernorm(h, axis=-1), L0_attn_Wq, L0_attn_Wk, L0_attn_Wv, L0_attn_Wo, L0_attn_bo, L0_attn_betas, L0_attn_mem, L0_attn_z)
    h = h + _L0_ffn_ref(_layernorm(h, axis=-1), L0_ffn_ln_gamma, L0_ffn_ln_beta, L0_ffn_router_w, L0_ffn_w12, L0_ffn_w3)
    return h

_drawn_inputs = setup_inputs


def setup_inputs(seed=0):
    import zlib

    import numpy as np

    out = dict(_drawn_inputs(seed))
    spreads = {'L0_attn_bo': (0.0, 0.8),
     'L0_attn_mem': (0.0, 0.1),
     'L0_attn_z': (0.0, 0.1),
     'L0_ffn_ln_gamma': (1.0, 0.6),
     'L0_ffn_ln_beta': (0.0, 0.8)}
    factors = {'L0_attn_Wk': 8.0,
     'L0_attn_Wv': 8.0,
     'L0_ffn_router_w': 8.0,
     'L0_ffn_w12': 7.843,
     'L0_ffn_w3': 7.934}
    for name, (base, spread) in spreads.items():
        noise = np.random.default_rng([zlib.crc32(name.encode()), seed]).standard_normal(out[name].shape)
        drawn = base * np.exp(spread * noise) if base else spread * noise
        out[name] = jnp.asarray(drawn.astype(out[name].dtype))
    for name, factor in factors.items():
        out[name] = (out[name] * factor).astype(out[name].dtype)
    return out
```

```python
from contextlib import ExitStack

import numpy as np
import concourse.bass as bass
from concourse import mybir

F32 = mybir.dt.float32
F32R = mybir.dt.float32r
U32 = mybir.dt.uint32
ALU = mybir.AluOpType
ACT = mybir.ActivationFunctionType
AX_X = mybir.AxisListType.X

P = 128
D = 256
KD = D // P
IMAGES, SIDE, PATCH, CHANNELS = 16, 96, 16, 3
NPATCH = (SIDE // PATCH) ** 2
S = NPATCH + 1
T = IMAGES * S
KE = PATCH * PATCH * CHANNELS // P
IMG_PER_GROUP = P // S
G_ROWS = IMG_PER_GROUP * S
GROUPS = -(-T // G_ROWS)
ROWS = [min(G_ROWS, T - g * G_ROWS) for g in range(GROUPS)]
HEADS, HD = 4, 64
HALF = T // 2
EXPERTS, TOPK = 8, 2
F = 1024
FC = F // P
CAP = -(-T * TOPK * 5 // (4 * EXPERTS))
CW = CAP + CAP % 2
TAIL = CW - P
PAIRS = EXPERTS // 2
EPS = 1e-5
FAR = 4096.0
MASKED = -3.0e38


def vit_tower(nc, xT, wpT, pos_bias_cls, wqkvoT, bo, betas, betas_by_row, mem, z, gamma, beta, routerT, w12T, w3T,
              c_sel, c_mask, c_before, c_ident, c_slots, c_token, c_dup, out):
    with ExitStack() as ctx:
        def sb(name, shape, dt=F32):
            return ctx.enter_context(nc.sbuf_tensor(name, shape, dt))

        def sem(name):
            return ctx.enter_context(nc.semaphore(name))

        bank = [ctx.enter_context(nc.psum_tensor(f"bank{i}", [P, 512], F32)) for i in range(8)]

        sel = sb("sel", [NPATCH + 2, T])
        pbc = sb("pbc", [NPATCH + 2, D])
        mask = sb("mask", [G_ROWS, G_ROWS])
        before = sb("before", [G_ROWS, G_ROWS])
        ones = sb("ones", [G_ROWS, G_ROWS])
        ident = sb("ident", [P, P])
        slot_iota = sb("slot_iota", [G_ROWS, CW])
        expert_iota = sb("expert_iota", [G_ROWS, EXPERTS])
        token_plus1 = sb("token_plus1", [G_ROWS, GROUPS])
        dup_far = sb("dup_far", [P, 4])
        x_sb = sb("x_sb", [P, KE, T])
        wp_sb = sb("wp_sb", [P, KE, D])
        w_sb = sb("w_sb", [P, 4, KD, D])
        bo_b = sb("bo_b", [G_ROWS, D])
        gamma_b = sb("gamma_b", [G_ROWS, D])
        beta_b = sb("beta_b", [G_ROWS, D])
        router_sb = sb("router_sb", [P, KD, EXPERTS])
        mem_bd = sb("mem_bd", [P, 2, P])
        z_bd = sb("z_bd", [P, 2, P])
        z_col = sb("z_col", [P, 2])
        beta_gate = sb("beta_gate", [P, 2])
        gate = sb("gate", [P, 2])
        beta_row = sb("beta_row", [G_ROWS, HEADS])
        keep = sb("keep", [G_ROWS, HEADS])

        h = sb("h", [G_ROWS, GROUPS, D])
        h_bo = sb("h_bo", [G_ROWS, GROUPS, D])
        hn = sb("hn", [G_ROWS, GROUPS, D])
        hnT = sb("hnT", [P, KD, T])
        v_sb = sb("v_sb", [G_ROWS, GROUPS, D])
        qT = sb("qT", [P, 2, T])
        kT = sb("kT", [P, 2, T])
        qneg = sb("qneg", [P, 2, T])
        qexp = qneg
        den = qneg
        sqT = sb("sqT", [P, 2, T])
        memT = sb("memT", [P, 2, T])
        scores = sb("scores", [G_ROWS, 2, HEADS, G_ROWS])
        probs = sb("probs", [G_ROWS, 2, HEADS, G_ROWS])
        pn = sb("pn", [G_ROWS, 2, HEADS, G_ROWS])
        probsT = sb("probsT", [G_ROWS, 2, HEADS, G_ROWS])
        negmax = sb("negmax", [G_ROWS, GROUPS, HEADS])
        psums = sb("psums", [G_ROWS, GROUPS, HEADS])
        aoT = sb("aoT", [P, 2, 2, G_ROWS])
        h2 = sb("h2", [G_ROWS, GROUPS, D])
        xg = hn
        xn = sb("xn", [G_ROWS, GROUPS, D])
        xn_hi = sb("xn_hi", [G_ROWS, GROUPS, D], F32R)
        xn_lo = sb("xn_lo", [G_ROWS, GROUPS, D], F32R)
        xnT = sb("xnT", [P, 2, KD, G_ROWS])
        stats = sb("stats", [G_ROWS, GROUPS, 6])
        mv1 = sb("mv1", [G_ROWS, GROUPS, 2])
        mv2 = sb("mv2", [G_ROWS, GROUPS, 2])
        std = sb("std", [G_ROWS, GROUPS])
        rstd = sb("rstd", [G_ROWS, GROUPS])
        eps_col = sb("eps_col", [G_ROWS, 1])

        logits = sb("logits", [G_ROWS, GROUPS, EXPERTS])
        top = sb("top", [G_ROWS, GROUPS, 8])
        top_i = sb("top_i", [G_ROWS, GROUPS, 8], U32)
        top_f = sb("top_f", [G_ROWS, GROUPS, 8])
        hot0 = sb("hot0", [G_ROWS, GROUPS, EXPERTS])
        hot1 = sb("hot1", [G_ROWS, GROUPS, EXPERTS])
        hot = sb("hot", [G_ROWS, GROUPS, EXPERTS])
        place = sb("place", [G_ROWS, EXPERTS, GROUPS])
        gap = sb("gap", [G_ROWS, GROUPS])
        e1 = sb("e1", [G_ROWS, GROUPS])
        p0 = sb("p0", [G_ROWS, GROUPS])
        p1 = sb("p1", [G_ROWS, GROUPS])
        wt = sb("wt", [G_ROWS, EXPERTS, GROUPS])
        wt1 = sb("wt1", [G_ROWS, EXPERTS, GROUPS])
        info = sb("info", [G_ROWS, EXPERTS, GROUPS, 4], F32R)

        pick = sb("pick", [G_ROWS, GROUPS, 2, CW], F32R)
        xb = sb("xb", [P, KD, 2, CW])
        w12 = [sb(f"w12_{b}", [P, KD, 2 * F]) for b in range(2)]
        w3 = [sb(f"w3_{b}", [P, FC, D]) for b in range(2)]
        sg = sb("sg", [P, 4, CW])
        x_flat = x_sb[:, :, :].rearrange("p k t -> p (k t)")
        hT = [x_flat[:, b * FC * CW:(b + 1) * FC * CW].rearrange("p (f c) -> p f c", f=FC) for b in range(2)]
        w_slot = sb("w_slot", [P, 4])
        t_far = sb("t_far", [P, 4])
        t_idx = sb("t_idx", [P, 4])
        slot_token = sb("slot_token", [P, 4], U32)
        yw = [wp_sb[:, n, :] for n in range(4)]

        in_embed = sem("in_embed")
        in_x = sem("in_x")
        in_attn = sem("in_attn")
        in_ffn = sem("in_ffn")
        bd_zero = sem("bd_zero")
        consts_set = sem("consts_set")
        embed_done = sem("embed_done")
        h_copied = sem("h_copied")
        h_bo_done = sem("h_bo_done")
        var1_done = sem("var1_done")
        std1_done = sem("std1_done")
        hn_done = sem("hn_done")
        hnT_in_psum = sem("hnT_in_psum")
        hnT_done = sem("hnT_done")
        v_in_psum = sem("v_in_psum")
        v_done = sem("v_done")
        qk_in_psum = sem("qk_in_psum")
        q_done = sem("q_done")
        k_done = sem("k_done")
        qneg_done = sem("qneg_done")
        qexp_done = sem("qexp_done")
        sq_done = sem("sq_done")
        gate_exp = sem("gate_exp")
        mem_in_psum = sem("mem_in_psum")
        mem_done = sem("mem_done")
        s_in_psum = sem("s_in_psum")
        masked = sem("masked")
        max_done = sem("max_done")
        exp_done = sem("exp_done")
        pn_done = sem("pn_done")
        pT_in_psum = sem("pT_in_psum")
        pT_done = sem("pT_done")
        pv_done = sem("pv_done")
        ao_done = sem("ao_done")
        wo_done = sem("wo_done")
        h2_done = sem("h2_done")
        h2_stored = sem("h2_stored")
        var2_done = sem("var2_done")
        std2_done = sem("std2_done")
        xn_done = sem("xn_done")
        xn_hi_done = sem("xn_hi_done")
        xn_lo_done = sem("xn_lo_done")
        xnT_in_psum = sem("xnT_in_psum")
        xnT_done = sem("xnT_done")
        logits_in_psum = sem("logits_in_psum")
        logits_read = sem("logits_read")
        hot_done = sem("hot_done")
        count_done = sem("count_done")
        place_done = sem("place_done")
        gap_done = sem("gap_done")
        e1_done = sem("e1_done")
        info_done = sem("info_done")
        dve_step = sem("dve_step")
        w12_in = [sem(f"w12_in{b}") for b in range(2)]
        w3_in = [sem(f"w3_in{b}") for b in range(2)]
        pick_done = sem("pick_done")
        gather_done = sem("gather_done")
        xb_done = sem("xb_done")
        slots_in_psum = sem("slots_in_psum")
        slots_stage = sem("slots_stage")
        slots_done = sem("slots_done")
        gu_done = sem("gu_done")
        silu_done = sem("silu_done")
        h_bank = [sem(f"h_bank{n}") for n in range(4)]
        y_done = sem("y_done")
        yw_done = [sem(f"yw_done{s}") for s in range(2)]
        yw_free = [sem(f"yw_free{n}") for n in range(4)]
        scattered = [sem(f"scattered{n}") for n in range(4)]

        def cols(g):
            return slice(g * G_ROWS, g * G_ROWS + ROWS[g])

        WIDE = [(m, n) for m in range(2) for n in range(2)]

        def half(n):
            return slice(n * HALF, (n + 1) * HALF)

        S_BANK = ((0, 1), (2, 3))
        PT_BANK = (4, 7)
        PV_BANK, WO_BANK = 5, 6
        LOGIT_BANK = (0, 1, 4, 5, 6, 7)
        PLACE_BANK = 2

        block = ctx.enter_context(nc.Block())

        @block.sync
        def _(sp):
            for n in range(4):
                sp.sem_inc(h_bank[n], 1)
                sp.sem_inc(yw_free[n], 1)
            for s in range(2):
                sp.sem_inc(yw_done[s], 1)
            sp.dma_start(sel[:, :], c_sel).then_inc(in_embed, 16)
            sp.dma_start(pbc[:, :], pos_bias_cls).then_inc(in_embed, 16)
            sp.dma_start(wp_sb[:, :, :], wpT).then_inc(in_embed, 16)
            sp.dma_start(ident[:, :], c_ident).then_inc(in_embed, 16)
            sp.dma_start(x_sb[:, :, :], xT).then_inc(in_x, 16)
            sp.dma_start(w_sb[:, :, :, :], wqkvoT).then_inc(in_attn, 16)
            sp.dma_start(mask[:, :], c_mask).then_inc(in_attn, 16)
            sp.dma_start(bo_b[:, :], bo.partition_broadcast(G_ROWS)).then_inc(in_attn, 16)
            sp.dma_start(beta_row[:, :], betas.partition_broadcast(G_ROWS)).then_inc(in_attn, 16)
            for hh in range(2):
                rows = slice(hh * HD, (hh + 1) * HD)
                sp.dma_start(beta_gate[rows, :], betas_by_row[hh].partition_broadcast(HD)).then_inc(in_attn, 16)
                sp.dma_start(z_col[rows, :], z[hh]).then_inc(in_attn, 16)
            sp.wait_ge(bd_zero, 1)
            for hh in range(2):
                rows = slice(hh * HD, (hh + 1) * HD)
                sp.dma_start(mem_bd[rows, :, rows], mem[hh]).then_inc(in_attn, 16)
            sp.dma_start(gamma_b[:, :], gamma.partition_broadcast(G_ROWS)).then_inc(in_ffn, 16)
            sp.dma_start(beta_b[:, :], beta.partition_broadcast(G_ROWS)).then_inc(in_ffn, 16)
            sp.dma_start(router_sb[:, :, :], routerT).then_inc(in_ffn, 16)
            sp.dma_start(before[:, :], c_before).then_inc(in_ffn, 16)
            sp.dma_start(slot_iota[:, :], c_slots.partition_broadcast(G_ROWS)).then_inc(in_ffn, 16)
            sp.dma_start(expert_iota[:, :], c_slots[0:EXPERTS].partition_broadcast(G_ROWS)).then_inc(in_ffn, 16)
            sp.dma_start(token_plus1[:, :], c_token).then_inc(in_ffn, 16)
            sp.dma_start(dup_far[:, :], c_dup).then_inc(in_ffn, 16)
            for b in range(2):
                sp.dma_start(w12[b][:, :, :], w12T[b]).then_inc(w12_in[b], 16)
                sp.dma_start(w3[b][:, :, :], w3T[b]).then_inc(w3_in[b], 16)
            for g in range(GROUPS):
                sp.wait_ge(h2_done, g + 1)
                sp.dma_start(out[g * G_ROWS:g * G_ROWS + ROWS[g], :], h2[0:ROWS[g], g, :]).then_inc(h2_stored, 16)
            with sp.Fori(1, PAIRS) as i:
                for b in range(2):
                    sp.wait_ge(gu_done, 2 * FC * i + (FC * (b + 1) - 2 * FC))
                    sp.dma_start(w12[b][:, :, :], w12T[bass.ds(2 * i + b, 1)].rearrange("o p k f -> p (o k) f")).then_inc(w12_in[b], 16)
                    sp.wait_ge(y_done, 4 * i + (2 * (b + 1) - 4))
                    sp.dma_start(w3[b][:, :, :], w3T[bass.ds(2 * i + b, 1)].rearrange("o p k d -> p (o k) d")).then_inc(w3_in[b], 16)
            for n in range(4):
                sp.wait_ge(scattered[n], 16 * PAIRS)
            sp.wait_ge(h2_stored, 16 * GROUPS)

        @block.tensor
        def _(pe):
            E_BANK, T_BANK, V_BANK = (0, 1), (2, 3), (4, 5)

            def embed(g):
                R = ROWS[g]
                if g == 0:
                    pe.wait_ge(in_embed, 64)
                if g >= 2:
                    pe.wait_ge(h_copied, g - 1)
                o = bank[E_BANK[g % 2]][0:R, 0:D]
                pe.matmul(o, sel[:, cols(g)], pbc[:, :], start=True, stop=False)
                if g == 0:
                    pe.wait_ge(in_x, 16)
                for k in range(KE):
                    mm = pe.matmul(o, x_sb[:, k, cols(g)], wp_sb[:, k, :], start=False, stop=(k == KE - 1))
                mm.then_inc(embed_done, 1)

            def turn_hn(g):
                R = ROWS[g]
                pe.wait_ge(hn_done, g + 1)
                if g >= 2:
                    pe.wait_ge(hnT_done, g - 1)
                for k in range(KD):
                    tr = pe.transpose(bank[T_BANK[g % 2]][:, k * P:k * P + R], hn[0:R, g, k * P:(k + 1) * P], ident[0:R, 0:R])
                tr.then_inc(hnT_in_psum, 1)

            def value(g):
                R = ROWS[g]
                pe.wait_ge(hnT_done, g + 1)
                if g == 0:
                    pe.wait_ge(in_attn, 160)
                if g >= 2:
                    pe.wait_ge(v_done, g - 1)
                for k in range(KD):
                    mm = pe.matmul(bank[V_BANK[g % 2]][0:R, 0:D], hnT[:, k, cols(g)], w_sb[:, 2, k, :],
                                   start=(k == 0), stop=(k == KD - 1))
                mm.then_inc(v_in_psum, 1)

            for t in range(GROUPS + 2):
                if t < GROUPS:
                    embed(t)
                if 1 <= t <= GROUPS:
                    turn_hn(t - 1)
                if t >= 2:
                    value(t - 2)

            QK_BANK = (0, 1, 6, 7)
            pe.wait_ge(h_copied, GROUPS)
            for which in range(2):
                for n, (m, hf) in enumerate(WIDE):
                    if which == 1:
                        pe.wait_ge(q_done, n + 1)
                    for k in range(KD):
                        mm = pe.matmul(bank[QK_BANK[n]][:, 0:HALF], w_sb[:, which, k, m * P:(m + 1) * P],
                                       hnT[:, k, half(hf)], start=(k == 0), stop=(k == KD - 1))
                    mm.then_inc(qk_in_psum, 1)

            def memory():
                for n, (m, hf) in enumerate(WIDE):
                    if n == 0:
                        pe.wait_ge(v_done, GROUPS)
                        pe.wait_ge(k_done, 4)
                    if n >= 2:
                        pe.wait_ge(mem_done, n - 1)
                    pe.wait_ge(sq_done, n + 1)
                    pe.matmul(bank[4 + n % 2][:, 0:HALF], z_bd[:, m, :], sqT[:, m, half(hf)], start=True, stop=True)
                    pe.matmul(bank[6 + n % 2][:, 0:HALF], mem_bd[:, m, :], sqT[:, m, half(hf)],
                              start=True, stop=True).then_inc(mem_in_psum, 1)

            def score(g):
                R = ROWS[g]
                if g >= 2:
                    pe.wait_ge(masked, 2 * g - 2)
                for hd in range(HEADS):
                    rows = slice(HD * (hd % 2), HD * (hd % 2) + HD)
                    mm = pe.matmul(bank[S_BANK[g % 2][hd % 2]][0:R, (hd // 2) * R:(hd // 2 + 1) * R], qT[rows, hd // 2, cols(g)],
                                   kT[rows, hd // 2, cols(g)], start=True, stop=True)
                mm.then_inc(s_in_psum, 1)

            def turn_probs(g):
                R = ROWS[g]
                pe.wait_ge(pn_done, g + 1)
                if g == 0:
                    pe.wait_ge(mem_done, 4)
                if g >= 2:
                    pe.wait_ge(pT_done, g - 1)
                for hd in range(HEADS):
                    tr = pe.transpose(bank[PT_BANK[g % 2]][0:R, hd * R:(hd + 1) * R], pn[0:R, g % 2, hd, 0:R], ident[0:R, 0:R])
                tr.then_inc(pT_in_psum, 1)

            def attend(g):
                R = ROWS[g]
                pe.wait_ge(pT_done, g + 1)
                if g >= 1:
                    pe.wait_ge(ao_done, g)
                for hd in range(HEADS):
                    rows = slice(HD * (hd % 2), HD * (hd % 2) + HD)
                    mm = pe.matmul(bank[PV_BANK][rows, (hd // 2) * R:(hd // 2 + 1) * R],
                                   v_sb[0:R, g, hd * HD:(hd + 1) * HD], probsT[0:R, g % 2, hd, 0:R], start=True, stop=True)
                mm.then_inc(pv_done, 1)

            def project(g):
                R = ROWS[g]
                pe.wait_ge(ao_done, g + 1)
                if g >= 1:
                    pe.wait_ge(h2_done, g)
                for k in range(2):
                    mm = pe.matmul(bank[WO_BANK][0:R, 0:D], aoT[:, g % 2, k, 0:R], w_sb[:, 3, k, :],
                                   start=(k == 0), stop=(k == 1))
                mm.then_inc(wo_done, 1)

            pe.wait_ge(k_done, 2)
            for t in range(GROUPS + 3):
                if t == 0:
                    pe.wait_ge(k_done, 4)
                if t < GROUPS:
                    score(t)
                if t == 0:
                    memory()
                if 1 <= t <= GROUPS:
                    turn_probs(t - 1)
                if 2 <= t <= GROUPS + 1:
                    attend(t - 2)
                if t >= 3:
                    project(t - 3)

            for g in range(GROUPS + 1):
                if g < GROUPS:
                    R = ROWS[g]
                    pe.wait_ge(xn_done, g + 1)
                    if g >= 2:
                        pe.wait_ge(xnT_done, g - 1)
                    for k in range(KD):
                        tr = pe.transpose(bank[2 + g % 2][:, k * P:k * P + R], xn[0:R, g, k * P:(k + 1) * P], ident[0:R, 0:R])
                    tr.then_inc(xnT_in_psum, 1)
                if g >= 1:
                    R = ROWS[g - 1]
                    pe.wait_ge(xnT_done, g)
                    for k in range(KD):
                        mm = pe.matmul(bank[LOGIT_BANK[g - 1]][0:R, 0:EXPERTS], xnT[:, (g - 1) % 2, k, 0:R],
                                       router_sb[:, k, :], start=(k == 0), stop=(k == KD - 1))
                    mm.then_inc(logits_in_psum, 1)

            pe.wait_ge(hot_done, 1)
            for g in range(GROUPS - 1):
                later = GROUPS - 1 - g
                pe.matmul(bank[PLACE_BANK][0:G_ROWS, (g + 1) * EXPERTS:GROUPS * EXPERTS].rearrange("p (g e) -> p g e", e=EXPERTS),
                          ones[:, :], hot[:, g:g + 1, :].broadcast_to([G_ROWS, later, EXPERTS]),
                          start=(g == 0), stop=False, skip_group_check=True)
            mm = pe.matmul(bank[PLACE_BANK][0:G_ROWS, 0:GROUPS * EXPERTS], before[:, :],
                           hot[:, :, :].rearrange("p g e -> p (g e)"), start=False, stop=True, skip_group_check=True)
            mm.then_inc(count_done, 1)

            def gather(i):
                pe.wait_ge(pick_done, 2 * i + 2)
                for k in range(KD):
                    o = bank[4 + k][:, 0:2 * CW]
                    for part, x in enumerate((xn_hi, xn_lo)):
                        for g in range(GROUPS):
                            R = ROWS[g]
                            mm = pe.matmul(o, x[0:R, g, k * P:(k + 1) * P], pick[0:R, g, :, :].rearrange("p b c -> p (b c)"),
                                           start=(part == 0 and g == 0), stop=(part == 1 and g == GROUPS - 1))
                    mm.then_inc(gather_done, 1)

            def slot_info(i):
                for b in range(2):
                    for s in range(2):
                        o = bank[5][:, 2 * CW + 4 * (2 * b + s):2 * CW + 4 * (2 * b + s) + 4]
                        for g in range(GROUPS):
                            R = ROWS[g]
                            mm = pe.matmul(o, pick[0:R, g, b, s * TAIL:s * TAIL + P],
                                           info[0:R, bass.ds(2 * i + b, 1), g, :].rearrange("p o c -> p (o c)"),
                                           start=(g == 0), stop=(g == GROUPS - 1))
                mm.then_inc(slots_in_psum, 1)

            def gate_up(i, b):
                pe.wait_ge(w12_in[b], 16 * i + 16)
                for fc in range(FC):
                    n = FC * b + fc
                    pe.wait_ge(h_bank[n % 4], 4 * i + n // 4 + 1)
                    for half_, off in ((0, 0), (1, F)):
                        for k in range(KD):
                            mm = pe.matmul(bank[n % 4][:, half_ * CW:half_ * CW + CW],
                                           w12[b][:, k, off + fc * P:off + (fc + 1) * P], xb[:, k, b, :],
                                           start=(k == 0), stop=(k == KD - 1))
                    mm.then_inc(gu_done, 1)

            def down(i, b):
                pe.wait_ge(w3_in[b], 16 * i + 16)
                for s in range(2):
                    pe.wait_ge(yw_done[s], 2 * i + b + 1)
                    for fc in range(FC):
                        if s == 0:
                            n = FC * b + fc
                            pe.wait_ge(h_bank[n % 4], 4 * i + n // 4 + 2)
                        mm = pe.matmul(bank[6 + s][:, 0:D], hT[b][:, fc, s * TAIL:s * TAIL + P], w3[b][:, fc, :],
                                       start=(fc == 0), stop=(fc == FC - 1))
                    mm.then_inc(y_done, 1)

            def pair(i, last):
                pe.wait_ge(xb_done, 2 * i + 2)
                pe.wait_ge(info_done, 1)
                slot_info(i)
                gate_up(i, 0)
                down(i, 0)
                gate_up(i, 1)
                if not last:
                    gather(i + 1)
                down(i, 1)

            pe.wait_ge(xn_hi_done, GROUPS)
            pe.wait_ge(xn_lo_done, GROUPS)
            gather(0)
            with pe.Fori(0, PAIRS - 1) as i:
                pair(i, False)
            pair(PAIRS - 1, True)

        @block.scalar
        def _(act):
            act.wait_ge(consts_set, 1)

            def copy_h(g):
                R = ROWS[g]
                act.wait_ge(embed_done, g + 1)
                act.activation(h[0:R, g, :], bank[g % 2][0:R, 0:D], ACT.Copy).then_inc(h_copied, 1)
                act.wait_ge(var1_done, g + 1)
                act.activation(std[0:R, g:g + 1], mv1[0:R, g, 1:2], ACT.Sqrt, bias=eps_col[0:R, :]).then_inc(std1_done, 1)

            def copy_hnT(g):
                R = ROWS[g]
                act.wait_ge(hnT_in_psum, g + 1)
                act.activation(hnT[:, :, cols(g)], bank[2 + g % 2][:, 0:2 * P].rearrange("p (k c) -> p k c", k=KD)[:, :, 0:R],
                               ACT.Copy).then_inc(hnT_done, 1)

            def copy_v(g):
                R = ROWS[g]
                act.wait_ge(v_in_psum, g + 1)
                act.activation(v_sb[0:R, g, :], bank[4 + g % 2][0:R, 0:D], ACT.Copy).then_inc(v_done, 1)

            for t in range(GROUPS + 2):
                if t < GROUPS:
                    copy_h(t)
                if 1 <= t <= GROUPS:
                    copy_hnT(t - 1)
                if t >= 2:
                    copy_v(t - 2)

            act.wait_ge(in_attn, 160)
            act.activation(gate[:, :], beta_gate[:, :], ACT.Exp, scale=-1.0).then_inc(gate_exp, 1)
            act.activation(keep[:, :], beta_row[:, :], ACT.Exp, scale=-1.0).then_inc(gate_exp, 1)
            QK_BANK = (0, 1, 6, 7)
            for n, (m, hf) in enumerate(WIDE):
                act.wait_ge(qk_in_psum, n + 1)
                act.activation(qT[:, m, half(hf)], bank[QK_BANK[n]][:, 0:HALF], ACT.Copy).then_inc(q_done, 1)
                act.wait_ge(qneg_done, n + 1)
                act.activation(qexp[:, m, half(hf)], qneg[:, m, half(hf)], ACT.Exp).then_inc(qexp_done, 1)
            for n, (m, hf) in enumerate(WIDE):
                act.wait_ge(qk_in_psum, 4 + n + 1)
                act.activation(kT[:, m, half(hf)], bank[QK_BANK[n]][:, 0:HALF], ACT.Copy).then_inc(k_done, 1)

            for t in range(GROUPS + 1):
                if t < GROUPS:
                    R = ROWS[t]
                    act.wait_ge(max_done, t + 1)
                    if t >= 2:
                        act.wait_ge(pn_done, t - 1)
                    for hd in range(HEADS):
                        a = act.activation(probs[0:R, t % 2, hd, 0:R], scores[0:R, t % 2, hd, 0:R], ACT.Exp,
                                           bias=negmax[0:R, t, hd:hd + 1], accum_out=psums[0:R, t, hd:hd + 1])
                    a.then_inc(exp_done, 1)
                if t >= 1:
                    g, R = t - 1, ROWS[t - 1]
                    act.wait_ge(pT_in_psum, g + 1)
                    if g >= 2:
                        act.wait_ge(pv_done, g - 1)
                    act.activation(probsT[0:R, g % 2, :, 0:R], bank[PT_BANK[g % 2]][0:R, 0:HEADS * R].rearrange("p (h c) -> p h c", h=HEADS),
                                   ACT.Copy).then_inc(pT_done, 1)

            act.wait_ge(var2_done, 1)
            act.activation(std[:, :], rstd[:, :], ACT.Sqrt).then_inc(std2_done, 1)
            for t in range(GROUPS + 1):
                if t < GROUPS:
                    R = ROWS[t]
                    act.wait_ge(xn_done, t + 1)
                    act.activation(xn_hi[0:R, t, :], xn[0:R, t, :], ACT.Copy).then_inc(xn_hi_done, 1)
                if t >= 1:
                    g, R = t - 1, ROWS[t - 1]
                    act.wait_ge(xnT_in_psum, g + 1)
                    if g >= 2:
                        act.wait_ge(logits_in_psum, g - 1)
                    act.activation(xnT[:, g % 2, :, 0:R], bank[2 + g % 2][:, 0:2 * P].rearrange("p (k c) -> p k c", k=KD)[:, :, 0:R],
                                   ACT.Copy).then_inc(xnT_done, 1)
            act.wait_ge(gap_done, 1)
            act.activation(e1[:, :], gap[:, :], ACT.Exp).then_inc(e1_done, 1)

            def take_tokens(i):
                for k in range(KD):
                    act.wait_ge(gather_done, 2 * i + k + 1)
                    act.activation(xb[:, k, :, :], bank[4 + k][:, 0:2 * CW].rearrange("p (b c) -> p b c", b=2),
                                   ACT.Copy).then_inc(xb_done, 1)

            def silu(i, b):
                for fc in range(FC):
                    n = FC * b + fc
                    act.wait_ge(gu_done, 2 * FC * i + n + 1)
                    act.activation(sg[:, n % 4, :], bank[n % 4][:, 0:CW], ACT.Silu).then_inc(silu_done, 1)

            def weigh(i, b):
                if b == 0:
                    act.wait_ge(slots_done, i + 1)
                for s in range(2):
                    act.wait_ge(y_done, 4 * i + 2 * b + s + 1)
                    act.wait_ge(yw_free[2 * b + s], i + 1)
                    act.activation(yw[2 * b + s], bank[6 + s][:, 0:D], ACT.Copy,
                                   scale=w_slot[:, 2 * b + s:2 * b + s + 1]).then_inc(yw_done[s], 1)

            def pair(i, last):
                silu(i, 0)
                weigh(i, 0)
                silu(i, 1)
                if not last:
                    take_tokens(i + 1)
                weigh(i, 1)

            take_tokens(0)
            with act.Fori(0, PAIRS - 1) as i:
                pair(i, False)
            pair(PAIRS - 1, True)

        @block.vector
        def _(dve):
            steps = [0]

            def then(ins):
                steps[0] += 1
                ins.then_inc(dve_step, 1)
                dve.wait_ge(dve_step, steps[0])

            dve.memset(eps_col[:, :], EPS).then_inc(consts_set, 1)
            dve.memset(mem_bd[:, :, :], 0.0).then_inc(bd_zero, 1)
            dve.memset(ones[:, :], 1.0)
            then(dve.memset(z_bd[:, :, :], 0.0))
            dve.memset(logits[:, :, :], 0.0)
            dve.memset(top[:, :, :], 0.0)
            dve.memset(top_i[:, :, :], 0)
            then(dve.memset(mv2[:, :, :], 1.0))
            then(dve.memset(info[:, :, :, :].bitcast(F32), 0.0))

            for g in range(GROUPS):
                R = ROWS[g]
                dve.wait_ge(h_copied, g + 1)
                then(dve.bn_stats(stats[0:R, g, :], h[0:R, g, :]))
                dve.bn_aggr(mv1[0:R, g, :], stats[0:R, g, :]).then_inc(var1_done, 1)
                dve.wait_ge(std1_done, g + 1)
                then(dve.reciprocal(rstd[0:R, g:g + 1], std[0:R, g:g + 1]))
                dve.tensor_scalar(hn[0:R, g, :], h[0:R, g, :], mv1[0:R, g, 0:1], rstd[0:R, g:g + 1],
                                  ALU.subtract, ALU.mult).then_inc(hn_done, 1)

            dve.wait_ge(in_attn, 160)
            for m in range(2):
                for hh in range(2):
                    rows = slice(hh * HD, (hh + 1) * HD)
                    dve.tensor_copy(z_bd[rows, m, rows], z_col[rows, m:m + 1].broadcast_to([HD, HD]))
            dve.wait_ge(gate_exp, 2)
            dve.tensor_scalar(gate[:, :], gate[:, :], 1.0, None, ALU.add)
            then(dve.tensor_scalar(keep[:, :], keep[:, :], 1.0, None, ALU.add))
            dve.reciprocal(gate[:, :], gate[:, :])
            then(dve.reciprocal(keep[:, :], keep[:, :]))
            then(dve.tensor_scalar(keep[:, :], keep[:, :], -1.0, 1.0, ALU.mult, ALU.add))

            for n, (m, hf) in enumerate(WIDE):
                dve.wait_ge(q_done, n + 1)
                dve.tensor_scalar(qneg[:, m, half(hf)], qT[:, m, half(hf)], 0.0, None, ALU.min).then_inc(qneg_done, 1)
            for n, (m, hf) in enumerate(WIDE):
                dve.wait_ge(qexp_done, n + 1)
                dve.scalar_tensor_tensor(out=sqT[:, m, half(hf)], in0=qT[:, m, half(hf)], scalar=0.0,
                                         in1=qexp[:, m, half(hf)], op0=ALU.max, op1=ALU.add).then_inc(sq_done, 1)

            def mask_and_max(g):
                R = ROWS[g]
                dve.wait_ge(s_in_psum, g + 1)
                if g >= 2:
                    dve.wait_ge(exp_done, g - 1)
                for hh in range(2):
                    dve.tensor_tensor(scores[0:R, g % 2, hh::2, 0:R],
                                      bank[S_BANK[g % 2][hh]][0:R, 0:2 * R].rearrange("p (h c) -> p h c", h=2),
                                      mask[0:R, 0:R].unsqueeze(1).broadcast_to([R, 2, R]), ALU.add).then_inc(masked, 1)
                dve.wait_ge(masked, 2 * g + 2)
                then(dve.tensor_reduce(negmax[0:R, g, :], scores[0:R, g % 2, :, 0:R], AX_X, ALU.max))
                dve.tensor_scalar(negmax[0:R, g, :], negmax[0:R, g, :], -1.0, None, ALU.mult).then_inc(max_done, 1)

            def memory_part(n, m, hf):
                dve.wait_ge(mem_in_psum, n + 1)
                then(dve.tensor_scalar(den[:, m, half(hf)], bank[4 + n % 2][:, 0:HALF], 1e-6, None, ALU.add))
                then(dve.reciprocal(den[:, m, half(hf)], den[:, m, half(hf)]))
                dve.scalar_tensor_tensor(out=memT[:, m, half(hf)], in0=bank[6 + n % 2][:, 0:HALF], scalar=gate[:, m:m + 1],
                                         in1=den[:, m, half(hf)], op0=ALU.mult, op1=ALU.mult).then_inc(mem_done, 1)

            def normalise(g):
                R = ROWS[g]
                dve.wait_ge(exp_done, g + 1)
                then(dve.reciprocal(psums[0:R, g, :], psums[0:R, g, :]))
                then(dve.tensor_tensor(psums[0:R, g, :], psums[0:R, g, :], keep[0:R, :], ALU.mult))
                if g >= 2:
                    dve.wait_ge(pT_in_psum, g - 1)
                dve.tensor_tensor(pn[0:R, g % 2, :, 0:R], probs[0:R, g % 2, :, 0:R],
                                  psums[0:R, g, :].unsqueeze(2).broadcast_to([R, HEADS, R]), ALU.mult).then_inc(pn_done, 1)

            def add_memory(g):
                R = ROWS[g]
                dve.wait_ge(pv_done, g + 1)
                if g == 0:
                    dve.wait_ge(mem_done, 4)
                if g >= 2:
                    dve.wait_ge(wo_done, g - 1)
                dve.tensor_tensor(aoT[:, g % 2, :, 0:R], bank[PV_BANK][:, 0:2 * R].rearrange("p (m c) -> p m c", m=2),
                                  memT[:, :, cols(g)], ALU.add).then_inc(ao_done, 1)

            def residual(g):
                R = ROWS[g]
                dve.wait_ge(wo_done, g + 1)
                dve.wait_ge(h_bo_done, g + 1)
                dve.tensor_tensor(h2[0:R, g, :], bank[WO_BANK][0:R, 0:D], h_bo[0:R, g, :], ALU.add).then_inc(h2_done, 1)
                dve.wait_ge(h2_done, g + 1)
                then(dve.bn_stats(stats[0:R, g, :], h2[0:R, g, :]))
                then(dve.bn_aggr(mv2[0:R, g, :], stats[0:R, g, :]))

            def choose(i, b):
                dve.tensor_tensor(pick[:, :, b, :], slot_iota[:, :].unsqueeze(1).broadcast_to([G_ROWS, GROUPS, CW]),
                                  place[:, bass.ds(2 * i + b, 1), :].rearrange("p o g -> p (o g)").unsqueeze(2).broadcast_to([G_ROWS, GROUPS, CW]),
                                  ALU.is_equal).then_inc(pick_done, 1)

            for t in range(GROUPS + 3):
                if t < GROUPS:
                    mask_and_max(t)
                if t == 0:
                    for n, (m, hf) in enumerate(WIDE):
                        memory_part(n, m, hf)
                if 1 <= t <= GROUPS:
                    normalise(t - 1)
                if 2 <= t <= GROUPS + 1:
                    add_memory(t - 2)
                if t >= 3:
                    residual(t - 3)

            dve.tensor_scalar(rstd[:, :], mv2[:, :, 1], 1.0 + EPS, EPS * EPS, ALU.mult, ALU.add).then_inc(var2_done, 1)
            dve.wait_ge(std2_done, 1)
            then(dve.reciprocal(rstd[:, :], std[:, :]))
            dve.wait_ge(in_ffn, 128)
            for g in range(GROUPS):
                R = ROWS[g]
                then(dve.scalar_tensor_tensor(out=xg[0:R, g, :], in0=h2[0:R, g, :], scalar=mv2[0:R, g, 0:1],
                                              in1=gamma_b[0:R, :], op0=ALU.subtract, op1=ALU.mult))
                dve.scalar_tensor_tensor(out=xn[0:R, g, :], in0=xg[0:R, g, :], scalar=rstd[0:R, g:g + 1],
                                         in1=beta_b[0:R, :], op0=ALU.mult, op1=ALU.add).then_inc(xn_done, 1)

            for g in range(GROUPS):
                R = ROWS[g]
                dve.wait_ge(logits_in_psum, g + 1)
                then(dve.tensor_scalar(logits[0:R, g, :], bank[LOGIT_BANK[g]][0:R, 0:EXPERTS], 1e4, -1e4, ALU.min, ALU.max))
                then(dve.max(top[0:R, g, :], logits[0:R, g, :]))
                then(dve.max_index(top_i[0:R, g, :], top[0:R, g, :], logits[0:R, g, :]))
            dve.tensor_tensor(gap[:, :], top[:, :, 1], top[:, :, 0], ALU.subtract).then_inc(gap_done, 1)
            then(dve.tensor_copy(top_f[:, :, :], top_i[:, :, :]))
            hots = expert_iota[:, :].unsqueeze(1).broadcast_to([G_ROWS, GROUPS, EXPERTS])
            dve.tensor_tensor(hot0[:, :, :], hots, top_f[:, :, 0:1].broadcast_to([G_ROWS, GROUPS, EXPERTS]), ALU.is_equal)
            then(dve.tensor_tensor(hot1[:, :, :], hots, top_f[:, :, 1:2].broadcast_to([G_ROWS, GROUPS, EXPERTS]), ALU.is_equal))
            R = ROWS[-1]
            then(dve.memset(hot[:, GROUPS - 1, :], 0.0))
            dve.tensor_tensor(hot[0:R, GROUPS - 1, :], hot0[0:R, GROUPS - 1, :], hot1[0:R, GROUPS - 1, :], ALU.add)
            dve.tensor_tensor(hot[:, 0:GROUPS - 1, :], hot0[:, 0:GROUPS - 1, :], hot1[:, 0:GROUPS - 1, :], ALU.add).then_inc(hot_done, 1)
            dve.wait_ge(count_done, 1)
            place_gp = place[:, :, :].rearrange("p e g -> p g e")
            then(dve.scalar_tensor_tensor(out=place_gp, in0=bank[PLACE_BANK][0:G_ROWS, 0:GROUPS * EXPERTS].rearrange("p (g e) -> p g e", e=EXPERTS),
                                          scalar=1.0, in1=hot[:, :, :], op0=ALU.add, op1=ALU.mult))
            dve.tensor_scalar(place[:, :, :], place[:, :, :], -1.0, None, ALU.add).then_inc(place_done, 1)
            dve.wait_ge(place_done, 1)
            choose(0, 0)
            choose(0, 1)
            dve.wait_ge(e1_done, 1)
            then(dve.tensor_scalar(p0[:, :], e1[:, :], 1.0, 1e-12, ALU.add, ALU.add))
            then(dve.reciprocal(p0[:, :], p0[:, :]))
            then(dve.tensor_tensor(p1[:, :], p0[:, :], e1[:, :], ALU.mult))
            wt_gp = wt[:, :, :].rearrange("p e g -> p g e")
            wt1_gp = wt1[:, :, :].rearrange("p e g -> p g e")
            dve.tensor_tensor(wt_gp, hot0[:, :, :], p0[:, :].unsqueeze(2).broadcast_to([G_ROWS, GROUPS, EXPERTS]), ALU.mult)
            then(dve.tensor_tensor(wt1_gp, hot1[:, :, :], p1[:, :].unsqueeze(2).broadcast_to([G_ROWS, GROUPS, EXPERTS]), ALU.mult))
            then(dve.tensor_tensor(wt[:, :, :], wt[:, :, :], wt1[:, :, :], ALU.add))
            dve.tensor_copy(info[:, :, :, 0], token_plus1[:, :].unsqueeze(1).broadcast_to([G_ROWS, EXPERTS, GROUPS]))
            then(dve.tensor_copy(info[:, :, :, 1], wt[:, :, :]))
            dve.tensor_tensor(info[:, :, :, 2], wt[:, :, :], info[:, :, :, 1].bitcast(F32), ALU.subtract).then_inc(info_done, 1)

            def hidden(i, b, fc):
                n = FC * b + fc
                dve.wait_ge(silu_done, 2 * FC * i + n + 1)
                dve.tensor_tensor(hT[b][:, fc, :], sg[:, n % 4, :], bank[n % 4][:, CW:2 * CW], ALU.mult).then_inc(h_bank[n % 4], 1)

            def slots(i):
                dve.wait_ge(slots_in_psum, i + 1)
                dve.wait_ge(yw_free[3], i + 1)
                o = bank[5][:, 2 * CW:2 * CW + 16].rearrange("p (n c) -> p n c", c=4)
                dve.tensor_copy(t_idx[:, :], o[:, :, 0])
                dve.tensor_copy(w_slot[:, :], o[:, :, 1]).then_inc(slots_stage, 1)
                dve.wait_ge(slots_stage, 4 * i + 1)
                dve.tensor_scalar(t_far[:, :], t_idx[:, :], 0.0, FAR, ALU.is_equal, ALU.mult)
                dve.tensor_tensor(w_slot[:, :], w_slot[:, :], o[:, :, 2], ALU.add).then_inc(slots_stage, 1)
                dve.wait_ge(slots_stage, 4 * i + 2)
                dve.scalar_tensor_tensor(out=t_idx[:, :], in0=t_idx[:, :], scalar=-1.0, in1=t_far[:, :],
                                         op0=ALU.add, op1=ALU.add).then_inc(slots_stage, 1)
                dve.wait_ge(slots_stage, 4 * i + 3)
                dve.tensor_tensor(t_idx[:, :], t_idx[:, :], dup_far[:, :], ALU.add).then_inc(slots_stage, 1)
                dve.wait_ge(slots_stage, 4 * i + 4)
                dve.tensor_copy(slot_token[:, :], t_idx[:, :]).then_inc(slots_done, 1)

            def pair(i, last):
                for b in range(2):
                    for fc in range(FC):
                        hidden(i, b, fc)
                        if b == 0 and fc == 3:
                            slots(i)
                        if b == 0 and fc in (4, 6) and not last:
                            choose(i + 1, (fc - 4) // 2)

            with dve.Fori(0, PAIRS - 1) as i:
                pair(i, False)
            pair(PAIRS - 1, True)

        @block.gpsimd
        def _(pool):
            pool.wait_ge(in_attn, 160)
            for g in range(GROUPS):
                R = ROWS[g]
                pool.wait_ge(h_copied, g + 1)
                pool.tensor_tensor(h_bo[0:R, g, :], h[0:R, g, :], bo_b[0:R, :], ALU.add).then_inc(h_bo_done, 1)
            for g in range(GROUPS):
                R = ROWS[g]
                pool.wait_ge(xn_hi_done, g + 1)
                pool.tensor_tensor(xn_lo[0:R, g, :], xn[0:R, g, :], xn_hi[0:R, g, :].bitcast(F32), ALU.subtract).then_inc(xn_lo_done, 1)

            def scatter(i, n):
                pool.wait_ge(yw_done[n % 2], 2 * i + n // 2 + 2)
                pool.indirect_dma_start(out=out, out_offset=bass.IndirectOffsetOnAxis(ap=slot_token[:, n:n + 1], axis=0),
                                        in_=yw[n], in_offset=None, bounds_check=T - 1, oob_is_err=False,
                                        compute_op=ALU.add).then_inc(scattered[n], 16)
                pool.wait_ge(scattered[n], 16 * i + 16)
                pool.sem_inc(yw_free[n], 1)

            pool.wait_ge(h2_stored, 16 * GROUPS)
            for i in range(PAIRS):
                pool.wait_ge(slots_done, i + 1)
                for n in range(4):
                    scatter(i, n)



def _constants():
    t = np.arange(T)
    sel = np.zeros((NPATCH + 2, T), np.float32)
    patch = t % S > 0
    sel[t[patch] % S - 1, t[patch]] = 1
    sel[NPATCH, t[patch]] = 1
    sel[NPATCH + 1, t[~patch]] = 1
    q = np.arange(G_ROWS)
    seen = (q[:, None] // S == q[None, :] // S) & (q[:, None] >= q[None, :])
    mask = np.where(seen, 0, MASKED).astype(np.float32)
    before = (q[:, None] < q[None, :]).astype(np.float32)
    slots = np.arange(CW, dtype=np.float32)
    slots[CAP:] = -2
    token = np.minimum(q[:, None] + G_ROWS * np.arange(GROUPS)[None, :] + 1, T).astype(np.float32)
    dup = np.zeros((P, 4), np.float32)
    dup[:P - TAIL, 1::2] = FAR
    return [sel, mask, before, np.eye(P, dtype=np.float32), slots, token, dup]


def kernel(x, cls_tok, L0_tok_W_proj, L0_tok_b_proj, L0_tok_pos_emb, L0_attn_Wq, L0_attn_Wk, L0_attn_Wv, L0_attn_Wo,
           L0_attn_bo, L0_attn_betas, L0_attn_mem, L0_attn_z, L0_ffn_ln_gamma, L0_ffn_ln_beta, L0_ffn_router_w,
           L0_ffn_w12, L0_ffn_w3):
    import concourse.bacc as bacc
    from concourse.bass_utils import run_bass_kernel_spmd

    side = SIDE // PATCH

    def to_partitions(a, k):
        return a.reshape(k, P, -1).transpose(1, 0, 2)

    patches = np.asarray(x).reshape(IMAGES, side, PATCH, side, PATCH, CHANNELS).transpose(0, 1, 3, 2, 4, 5).reshape(IMAGES, NPATCH, -1)
    tokens = np.pad(patches, ((0, 0), (1, 0), (0, 0))).reshape(T, -1)
    mem = np.asarray(L0_attn_mem).reshape(2, 2, HD, HD).transpose(1, 2, 0, 3)
    z = np.asarray(L0_attn_z).reshape(2, 2, HD).transpose(1, 2, 0)
    weights = [np.asarray(w).T for w in (L0_attn_Wq, L0_attn_Wk, L0_attn_Wv, L0_attn_Wo)]
    arrays = [
        to_partitions(tokens.T, KE),
        to_partitions(np.asarray(L0_tok_W_proj).T, KE),
        np.concatenate([np.asarray(L0_tok_pos_emb), np.asarray(L0_tok_b_proj)[None], np.asarray(cls_tok)[0]]),
        np.stack([to_partitions(w, KD) for w in weights], axis=1),
        np.asarray(L0_attn_bo), np.asarray(L0_attn_betas).reshape(HEADS), np.asarray(L0_attn_betas).reshape(2, 2).T, mem, z,
        np.asarray(L0_ffn_ln_gamma), np.asarray(L0_ffn_ln_beta),
        to_partitions(np.asarray(L0_ffn_router_w).T, KD),
        np.asarray(L0_ffn_w12).transpose(0, 2, 1).reshape(EXPERTS, KD, P, 2 * F).transpose(0, 2, 1, 3),
        np.asarray(L0_ffn_w3).transpose(0, 2, 1).reshape(EXPERTS, FC, P, D).transpose(0, 2, 1, 3),
    ] + _constants()

    nc = bacc.Bacc("TRN2", target_bir_lowering=False, num_devices=1)
    inputs, args = {}, []
    for n, a in enumerate(arrays):
        a = np.ascontiguousarray(a)
        inputs[f"in{n}"] = a
        args.append(nc.dram_tensor(f"in{n}", a.shape, mybir.dt.from_np(a.dtype), kind="ExternalInput").ap())
    args.append(nc.dram_tensor("out", (T, D), F32, kind="ExternalOutput").ap())
    vit_tower(nc, *args)
    r = run_bass_kernel_spmd(nc, [inputs], core_ids=[0])
    return r.results[0]["out"].reshape(IMAGES, S, D)
```

```python
from contextlib import ExitStack

import numpy as np
import concourse.bass as bass
from concourse import mybir

F32 = mybir.dt.float32
F32R = mybir.dt.float32r
BF16 = mybir.dt.bfloat16
U32 = mybir.dt.uint32
ALU = mybir.AluOpType
ACT = mybir.ActivationFunctionType
AX_X = mybir.AxisListType.X

P = 128
D = 256
KD = D // P
IMAGES, SIDE, PATCH, CHANNELS = 16, 96, 16, 3
NPATCH = (SIDE // PATCH) ** 2
S = NPATCH + 1
T = IMAGES * S
KE = PATCH * PATCH * CHANNELS // P
IMG_PER_GROUP = P // S
G_ROWS = IMG_PER_GROUP * S
GROUPS = -(-T // G_ROWS)
ROWS = [min(G_ROWS, T - g * G_ROWS) for g in range(GROUPS)]
HEADS, HD = 4, 64
HALF = T // 2
EXPERTS, TOPK = 8, 2
F = 1024
FC = F // P
CAP = -(-T * TOPK * 5 // (4 * EXPERTS))
CW = 192
TAIL = CW - P
PAIRS = EXPERTS // 2
EPS = 1e-5
W12_PARTS = 4
W12_PART = KD * 2 * F // W12_PARTS
FAR = 4096.0
MASKED = -3.0e38


def vit_tower(nc, xT, wpT, pos_cls, bias_rows, wqkvoT, bo, betas, mem_diag, z4, gamma, beta, routerT, w12T, w3T,
              c_mask, c_before, c_ident, c_slots, c_token, c_dup, c_head, out):
    with ExitStack() as ctx:
        def sb(name, shape, dt=F32):
            return ctx.enter_context(nc.sbuf_tensor(name, shape, dt))

        def sem(name):
            return ctx.enter_context(nc.semaphore(name))

        bank = [ctx.enter_context(nc.psum_tensor(f"bank{i}", [P, 512], F32)) for i in range(8)]

        ident = sb("ident", [P, P])
        slot_iota = sb("slot_iota", [G_ROWS, CW])
        expert_iota = sb("expert_iota", [G_ROWS, EXPERTS])
        token_plus1 = sb("token_plus1", [G_ROWS, GROUPS])
        dup_far = sb("dup_far", [P, 2])
        h2 = sb("h2", [G_ROWS, GROUPS, D])
        xn_hi = sb("xn_hi", [G_ROWS, GROUPS, D], F32R)
        xn_lo = sb("xn_lo", [G_ROWS, GROUPS, D], F32R)
        logits = sb("logits", [G_ROWS, GROUPS, EXPERTS])
        top = sb("top", [G_ROWS, GROUPS, 8])
        top_i = sb("top_i", [G_ROWS, GROUPS, 8], U32)
        top_f = sb("top_f", [G_ROWS, GROUPS, 8])
        hot0 = sb("hot0", [G_ROWS, GROUPS, EXPERTS])
        hot1 = sb("hot1", [G_ROWS, GROUPS, EXPERTS])
        hot = sb("hot", [G_ROWS, GROUPS, EXPERTS])
        place = sb("place", [G_ROWS, EXPERTS, GROUPS])
        gap = sb("gap", [G_ROWS, GROUPS])
        e1 = sb("e1", [G_ROWS, GROUPS])
        p0 = sb("p0", [G_ROWS, GROUPS])
        p1 = sb("p1", [G_ROWS, GROUPS])
        wt = sb("wt", [G_ROWS, EXPERTS, GROUPS])
        wt1 = sb("wt1", [G_ROWS, EXPERTS, GROUPS])
        info = sb("info", [G_ROWS, EXPERTS, GROUPS, 4], F32R)
        w12 = [sb(f"w12_{b}", [P, KD * 2 * F]) for b in range(2)]
        w3 = [sb(f"w3_{b}", [P, FC * D]) for b in range(2)]

        def split_buffers(b):
            return [sb(f"{n}_{b}", [P, size], F32R) for n, size in
                    (("w12_hi", KD * 2 * F), ("w12_lo", KD * 2 * F), ("w3_hi", FC * D), ("w3_lo", FC * D))]

        w_split = [split_buffers(0)]

        dense = ExitStack()

        def sb1(name, shape, dt=F32):
            return dense.enter_context(nc.sbuf_tensor(name, shape, dt))

        pos = sb1("pos", [G_ROWS, D])
        bias = sb1("bias", [G_ROWS, D])
        ident_bf = sb1("ident_bf", [G_ROWS, G_ROWS], BF16)
        mask_bf = sb1("mask_bf", [G_ROWS, G_ROWS], BF16)
        mask = sb1("mask", [G_ROWS, G_ROWS])
        before = sb1("before", [G_ROWS, G_ROWS])
        ones = sb1("ones", [G_ROWS, G_ROWS])
        x_flat = sb1("x_flat", [P, GROUPS * KE * G_ROWS])
        x_sb = x_flat[:, :].rearrange("p (g k c) -> p g k c", g=GROUPS, k=KE)
        x_taken = [0]

        def in_x_space(rows, a, b, c):
            start = x_taken[0]
            x_taken[0] += a * b * c
            return x_flat[0:rows, start:start + a * b * c].rearrange("p (a b c) -> p a b c", a=a, b=b)

        wp_sb = sb1("wp_sb", [P, KE, D])
        w_sb = sb1("w_sb", [P, 4, KD, D])
        bo_b = sb1("bo_b", [G_ROWS, D])
        gamma_b = sb1("gamma_b", [G_ROWS, D])
        beta_b = sb1("beta_b", [G_ROWS, D])
        router_sb = sb1("router_sb", [P, KD, EXPERTS])
        mem_bd = sb1("mem_bd", [P, 2, P])
        z_sb = sb1("z_sb", [P, 2, HEADS])
        head_rows = sb1("head_rows", [2 * HEADS, 2, P])
        head_rows_r = sb1("head_rows_r", [2 * HEADS, 2, P], F32R)
        gate = sb1("gate", [G_ROWS, HEADS])
        keep = sb1("keep", [G_ROWS, HEADS])
        h = sb1("h", [G_ROWS, GROUPS, D])
        hn = sb1("hn", [G_ROWS, GROUPS, D])
        hnT = sb1("hnT", [P, KD, T])
        v_sb = sb1("v_sb", [G_ROWS, GROUPS, D])
        qT = sb1("qT", [P, 2, T])
        kT = sb1("kT", [P, 2, T])
        qneg = sb1("qneg", [P, 2, T])
        sqT = sb1("sqT", [P, 2, T])
        memT = qneg
        den = sb1("den", [G_ROWS, GROUPS, HEADS])
        den_split = sb1("den_split", [G_ROWS, GROUPS, 2, HEADS], F32R)
        denT = sb1("denT", [2 * HEADS, T], F32R)
        memgate = in_x_space(P, 1, 2, HALF)[:, 0]
        probs = in_x_space(G_ROWS, 2, HEADS, G_ROWS)
        probsT = in_x_space(G_ROWS, 2, HEADS, G_ROWS)
        negmax = sb1("negmax", [G_ROWS, GROUPS, HEADS])
        psums = sb1("psums", [G_ROWS, GROUPS, HEADS])
        aoT = in_x_space(P, 2, 2, G_ROWS)
        xg = hn
        xn = hn
        xnT = sb1("xnT", [P, 2, KD, G_ROWS])
        stats = sb1("stats", [G_ROWS, GROUPS, 6])
        mv1 = sb1("mv1", [G_ROWS, GROUPS, 2])
        mv2 = sb1("mv2", [G_ROWS, GROUPS, 2])
        var1 = sb1("var1", [G_ROWS, GROUPS])
        var2 = sb1("var2", [G_ROWS, GROUPS])
        rstd1 = sb1("rstd1", [G_ROWS, GROUPS])
        rstd2 = sb1("rstd2", [G_ROWS, GROUPS])
        minus_half = sb1("minus_half", [G_ROWS, 1])
        dense.close()

        w_split.append(split_buffers(1))
        pick = sb("pick", [G_ROWS, GROUPS, CW], F32R)
        xb = sb("xb", [P, KD, 2, CW], F32R)
        sg = sb("sg", [P, 4, CW])
        hid = sb("hid", [P, 4, CW])
        hid_hi = sb("hid_hi", [P, FC, CW], F32R)
        hid_lo = sb("hid_lo", [P, FC, CW], F32R)
        slot_row = sb("slot_row", [P, 2])
        slot_far = sb("slot_far", [P, 2])
        w_slot = sb("w_slot", [P, 2])
        slot_token = [sb(f"slot_token{b}", [P, 2], U32) for b in range(2)]
        yw = [sb(f"yw_{n}", [P, D]) for n in range(4)]

        in_embed = sem("in_embed")
        in_x = [sem(f"in_x{g}") for g in range(GROUPS)]
        in_ident = sem("in_ident")
        in_pos = sem("in_pos")
        pos_done = sem("pos_done")
        in_attn = sem("in_attn")
        in_ffn = sem("in_ffn")
        consts_set = sem("consts_set")
        embed_done = sem("embed_done")
        h_copied = sem("h_copied")
        h_bo_done = sem("h_bo_done")
        var1_done = sem("var1_done")
        rstd1_done = sem("rstd1_done")
        hn_done = sem("hn_done")
        hnT_in_psum = sem("hnT_in_psum")
        hnT_done = sem("hnT_done")
        v_in_psum = sem("v_in_psum")
        v_done = sem("v_done")
        qk_in_psum = sem("qk_in_psum")
        q_done = sem("q_done")
        k_done = sem("k_done")
        qneg_done = sem("qneg_done")
        qexp_done = sem("qexp_done")
        sq_done = sem("sq_done")
        gate_exp = sem("gate_exp")
        gate_done = sem("gate_done")
        den_in_psum = sem("den_in_psum")
        den_done = sem("den_done")
        denT_in_psum = sem("denT_in_psum")
        denT_done = sem("denT_done")
        mem_in_psum = sem("mem_in_psum")
        memgate_done = sem("memgate_done")
        mem_done = sem("mem_done")
        s_in_psum = sem("s_in_psum")
        mask_set = sem("mask_set")
        max_done = sem("max_done")
        exp_done = sem("exp_done")
        pn_done = sem("pn_done")
        pT_in_psum = sem("pT_in_psum")
        pT_done = sem("pT_done")
        pv_done = sem("pv_done")
        ao_done = sem("ao_done")
        wo_done = sem("wo_done")
        h2_done = sem("h2_done")
        h2_stored = sem("h2_stored")
        var2_done = sem("var2_done")
        rstd2_done = sem("rstd2_done")
        xn_done = sem("xn_done")
        xn_hi_done = sem("xn_hi_done")
        xn_lo_done = sem("xn_lo_done")
        xnT_in_psum = sem("xnT_in_psum")
        xnT_done = sem("xnT_done")
        logits_in_psum = sem("logits_in_psum")
        logits_read = sem("logits_read")
        hot_done = sem("hot_done")
        count_done = sem("count_done")
        place_done = sem("place_done")
        gap_done = sem("gap_done")
        e1_done = sem("e1_done")
        info_done = sem("info_done")
        dve_step = sem("dve_step")
        w12_in = [sem(f"w12_in{b}") for b in range(2)]
        w3_in = [sem(f"w3_in{b}") for b in range(2)]
        pick_done = sem("pick_done")
        gather_done = sem("gather_done")
        xb_done = sem("xb_done")
        slots_in_psum = sem("slots_in_psum")
        slots_stage = sem("slots_stage")
        slots_done = sem("slots_done")
        gu_done = sem("gu_done")
        silu_done = sem("silu_done")
        w12_hi_done = sem("w12_hi_done")
        w12_lo_done = [sem(f"w12_lo_done_{who}") for who in ("dve", "pool")]
        w3_hi_done = sem("w3_hi_done")
        w3_lo_done = sem("w3_lo_done")
        hid_hi_done = sem("hid_hi_done")
        hid_lo_done = sem("hid_lo_done")
        h_bank = [sem(f"h_bank{n}") for n in range(4)]
        y_done = sem("y_done")
        yw_done = [sem(f"yw_done{s}") for s in range(2)]
        yw_free = [sem(f"yw_free{n}") for n in range(4)]
        scattered = [sem(f"scattered{n}") for n in range(4)]

        def cols(g):
            return slice(g * G_ROWS, g * G_ROWS + ROWS[g])

        WIDE = [(m, n) for m in range(2) for n in range(2)]

        def half(n):
            return slice(n * HALF, (n + 1) * HALF)

        S_BANK = ((0, 1), (2, 3))
        PT_BANK = 4
        PV_BANK, WO_BANK = 5, 6
        ROUTER_BANK = 7
        PLACE_BANK = 3

        block = ctx.enter_context(nc.Block())

        @block.sync
        def _(sp):
            for n in range(4):
                sp.sem_inc(h_bank[n], 1)
                sp.sem_inc(yw_free[n], 1)
            for s in range(2):
                sp.sem_inc(yw_done[s], 1)
            sp.sem_inc(hid_lo_done, 4)
            for g in range(GROUPS):
                sp.dma_start(x_sb[:, g, :, :], xT[g]).then_inc(in_x[g], 16)
                if g == 0:
                    sp.dma_start(pos[:, :], pos_cls).then_inc(in_pos, 16)
                    sp.dma_start(bias[:, :], bias_rows).then_inc(in_pos, 16)
            sp.dma_start(mask[:, :], c_mask).then_inc(in_attn, 16)
            sp.dma_start(bo_b[:, :], bo.partition_broadcast(G_ROWS)).then_inc(in_attn, 16)
            sp.dma_start(gate[:, :], betas.partition_broadcast(G_ROWS)).then_inc(in_attn, 16)
            sp.dma_start(z_sb[:, :, :], z4).then_inc(in_attn, 16)
            sp.dma_start(mem_bd[:, :, :], mem_diag).then_inc(in_attn, 16)
            sp.dma_start(head_rows[:, :, :], c_head).then_inc(in_attn, 16)
            for b in range(2):
                sp.dma_start(w12[b][:, :], w12T[b]).then_inc(w12_in[b], 16)
                sp.dma_start(w3[b][:, :], w3T[b]).then_inc(w3_in[b], 16)
                if b == 0:
                    sp.dma_start(gamma_b[:, :], gamma.partition_broadcast(G_ROWS)).then_inc(in_ffn, 16)
                    sp.dma_start(beta_b[:, :], beta.partition_broadcast(G_ROWS)).then_inc(in_ffn, 16)
                    sp.dma_start(router_sb[:, :, :], routerT).then_inc(in_ffn, 16)
                    sp.dma_start(before[:, :], c_before).then_inc(in_ffn, 16)
                    sp.dma_start(slot_iota[:, :], c_slots.partition_broadcast(G_ROWS)).then_inc(in_ffn, 16)
                    sp.dma_start(expert_iota[:, :], c_slots[0:EXPERTS].partition_broadcast(G_ROWS)).then_inc(in_ffn, 16)
                    sp.dma_start(token_plus1[:, :], c_token).then_inc(in_ffn, 16)
                    sp.dma_start(dup_far[:, :], c_dup).then_inc(in_ffn, 16)
            for g in range(GROUPS):
                sp.wait_ge(h2_done, g + 1)
                sp.dma_start(out[g * G_ROWS:g * G_ROWS + ROWS[g], :], h2[0:ROWS[g], g, :]).then_inc(h2_stored, 16)
            with sp.Fori(1, PAIRS) as i:
                for b in range(2):
                    sp.wait_ge(w12_lo_done[0], 4 * i + 2 * (b + 1) - 4)
                    sp.wait_ge(w12_lo_done[1], 4 * i + 2 * (b + 1) - 4)
                    sp.dma_start(w12[b][:, :], w12T[bass.ds(2 * i + b, 1)].rearrange("o p n -> (o p) n")).then_inc(w12_in[b], 16)
                    sp.wait_ge(w3_lo_done, 2 * i + b + 1 - 2)
                    sp.dma_start(w3[b][:, :], w3T[bass.ds(2 * i + b, 1)].rearrange("o p n -> (o p) n")).then_inc(w3_in[b], 16)
            for n in range(4):
                sp.wait_ge(scattered[n], 16 * PAIRS)
            sp.wait_ge(h2_stored, 16 * GROUPS)

        @block.tensor
        def _(pe):
            E_BANK, T_BANK, V_BANK = (0, 1), (2, 3), (4, 5)

            def embed(g):
                R = ROWS[g]
                if g == 0:
                    pe.wait_ge(in_embed, 16)
                if g >= 2:
                    pe.wait_ge(h_copied, g - 1)
                o = bank[E_BANK[g % 2]][0:R, 0:D]
                pe.wait_ge(in_x[g], 16)
                for k in range(KE):
                    mm = pe.matmul(o, x_sb[:, g, k, 0:R], wp_sb[:, k, :], start=(k == 0), stop=(k == KE - 1))
                mm.then_inc(embed_done, 1)

            def turn_hn(g):
                R = ROWS[g]
                if g == 0:
                    pe.wait_ge(in_ident, 16)
                pe.wait_ge(hn_done, g + 1)
                if g >= 2:
                    pe.wait_ge(hnT_done, g - 1)
                for k in range(KD):
                    tr = pe.transpose(bank[T_BANK[g % 2]][:, k * P:k * P + R], hn[0:R, g, k * P:(k + 1) * P], ident[0:R, 0:R])
                tr.then_inc(hnT_in_psum, 1)

            def value(g):
                R = ROWS[g]
                pe.wait_ge(hnT_done, g + 1)
                if g == 0:
                    pe.wait_ge(in_attn, 112)
                if g >= 2:
                    pe.wait_ge(v_done, g - 1)
                for k in range(KD):
                    mm = pe.matmul(bank[V_BANK[g % 2]][0:R, 0:D], hnT[:, k, cols(g)], w_sb[:, 2, k, :],
                                   start=(k == 0), stop=(k == KD - 1))
                mm.then_inc(v_in_psum, 1)

            for t in range(GROUPS + 2):
                if t < GROUPS:
                    embed(t)
                if 1 <= t <= GROUPS:
                    turn_hn(t - 1)
                if t >= 2:
                    value(t - 2)

            QK_BANK = (0, 1, 6, 7)
            pe.wait_ge(h_copied, GROUPS)
            for which in range(2):
                for n, (m, hf) in enumerate(WIDE):
                    if which == 1:
                        pe.wait_ge(q_done, n + 1)
                    for k in range(KD):
                        mm = pe.matmul(bank[QK_BANK[n]][:, 0:HALF], w_sb[:, which, k, m * P:(m + 1) * P],
                                       hnT[:, k, half(hf)], start=(k == 0), stop=(k == KD - 1))
                    mm.then_inc(qk_in_psum, 1)

            def memory_den():
                pe.wait_ge(v_done, GROUPS)
                for g in range(GROUPS):
                    R = ROWS[g]
                    for m in range(2):
                        if g == 0 or cols(g - 1).stop <= HALF < cols(g).stop:
                            pe.wait_ge(sq_done, (1 if g == 0 else 2) + 2 * m)
                        mm = pe.matmul(bank[4][0:R, g * HEADS:(g + 1) * HEADS], sqT[:, m, cols(g)], z_sb[:, m, :],
                                       start=(m == 0), stop=(m == 1))
                mm.then_inc(den_in_psum, 1)

            def memory_turn():
                pe.wait_ge(den_done, 1)
                for g in range(GROUPS):
                    R = ROWS[g]
                    b, c = g // (GROUPS // 2), g % (GROUPS // 2) * G_ROWS
                    tr = pe.transpose(bank[4 + b][0:2 * HEADS, c:c + R],
                                      den_split[0:R, g, :, :].bitcast(F32).rearrange("p s h -> p (s h)"), ident[0:R, 0:R])
                tr.then_inc(denT_in_psum, 1)

            def memory():
                pe.wait_ge(denT_done, 2)
                for n, (m, hf) in enumerate(WIDE):
                    if n == 0:
                        pe.wait_ge(k_done, 4)
                    if n >= 2:
                        pe.wait_ge(mem_done, n - 1)
                    pe.matmul(bank[4 + n % 2][:, 0:HALF], head_rows_r[:, m, :], denT[:, half(hf)], start=True, stop=True)
                    pe.matmul(bank[6 + n % 2][:, 0:HALF], mem_bd[:, m, :], sqT[:, m, half(hf)],
                              start=True, stop=True).then_inc(mem_in_psum, 1)

            def score(g):
                R = ROWS[g]
                if g >= 2:
                    pe.wait_ge(exp_done, g - 1)
                for hh in range(2):
                    pe.matmul(bank[S_BANK[g % 2][hh]][0:R, 0:2 * R].rearrange("p (h c) -> p h c", h=2), ident_bf[:, 0:R],
                              mask_bf[:, 0:R].unsqueeze(1).broadcast_to([G_ROWS, 2, R]), start=True, stop=False, skip_group_check=True)
                for hd in range(HEADS):
                    rows = slice(HD * (hd % 2), HD * (hd % 2) + HD)
                    mm = pe.matmul(bank[S_BANK[g % 2][hd % 2]][0:R, (hd // 2) * R:(hd // 2 + 1) * R], qT[rows, hd // 2, cols(g)],
                                   kT[rows, hd // 2, cols(g)], start=False, stop=True, skip_group_check=True)
                mm.then_inc(s_in_psum, 1)

            def turn_probs(g):
                R = ROWS[g]
                pe.wait_ge(pn_done, g + 1)
                if g == 0:
                    pe.wait_ge(mem_done, 4)
                if g >= 1:
                    pe.wait_ge(pT_done, g)
                for hd in range(HEADS):
                    tr = pe.transpose(bank[PT_BANK][0:R, hd * R:(hd + 1) * R], probs[0:R, g % 2, hd, 0:R], ident[0:R, 0:R])
                tr.then_inc(pT_in_psum, 1)

            def attend(g):
                R = ROWS[g]
                pe.wait_ge(pT_done, g + 1)
                if g >= 1:
                    pe.wait_ge(ao_done, g)
                for hd in range(HEADS):
                    rows = slice(HD * (hd % 2), HD * (hd % 2) + HD)
                    mm = pe.matmul(bank[PV_BANK][rows, (hd // 2) * R:(hd // 2 + 1) * R],
                                   v_sb[0:R, g, hd * HD:(hd + 1) * HD], probsT[0:R, g % 2, hd, 0:R], start=True, stop=True)
                mm.then_inc(pv_done, 1)

            def project(g):
                R = ROWS[g]
                pe.wait_ge(ao_done, g + 1)
                if g >= 1:
                    pe.wait_ge(h2_done, g)
                for k in range(2):
                    mm = pe.matmul(bank[WO_BANK][0:R, 0:D], aoT[:, g % 2, k, 0:R], w_sb[:, 3, k, :],
                                   start=(k == 0), stop=(k == 1))
                mm.then_inc(wo_done, 1)

            def turn_xn(g):
                R = ROWS[g]
                pe.wait_ge(xn_done, g + 1)
                if g >= 1:
                    pe.wait_ge(logits_read, g)
                for k in range(KD):
                    tr = pe.transpose(bank[ROUTER_BANK][:, k * P:k * P + R], xn[0:R, g, k * P:(k + 1) * P], ident[0:R, 0:R])
                tr.then_inc(xnT_in_psum, 1)

            def route(g):
                R = ROWS[g]
                pe.wait_ge(xnT_done, g + 1)
                for k in range(KD):
                    mm = pe.matmul(bank[ROUTER_BANK][0:R, 2 * P:2 * P + EXPERTS], xnT[:, g % 2, k, 0:R],
                                   router_sb[:, k, :], start=(k == 0), stop=(k == KD - 1))
                mm.then_inc(logits_in_psum, 1)

            memory_den()
            pe.wait_ge(k_done, 4)
            pe.wait_ge(mask_set, 1)
            score(0)
            score(1)
            memory_turn()
            memory()
            for t in range(GROUPS + 7):
                for lag, stage in ((6, route), (0, score), (3, attend), (4, project), (2, turn_probs), (5, turn_xn)):
                    if 0 <= t - lag < GROUPS and not (stage == score and t < 2):
                        stage(t - lag)

            pe.wait_ge(hot_done, 1)
            for g in range(GROUPS - 1):
                later = GROUPS - 1 - g
                pe.matmul(bank[PLACE_BANK][0:G_ROWS, (g + 1) * EXPERTS:GROUPS * EXPERTS].rearrange("p (g e) -> p g e", e=EXPERTS),
                          ones[:, :], hot[:, g:g + 1, :].broadcast_to([G_ROWS, later, EXPERTS]),
                          start=(g == 0), stop=False, skip_group_check=True)
            mm = pe.matmul(bank[PLACE_BANK][0:G_ROWS, 0:GROUPS * EXPERTS], before[:, :],
                           hot[:, :, :].rearrange("p g e -> p (g e)"), start=False, stop=True, skip_group_check=True)
            mm.then_inc(count_done, 1)

            def gather(i, b):
                pe.wait_ge(pick_done, 2 * i + b + 1)
                for k in range(KD):
                    for part, x in enumerate((xn_hi, xn_lo)):
                        for g in range(GROUPS):
                            R = ROWS[g]
                            mm = pe.matmul(bank[4 + k][:, part * CW:(part + 1) * CW], x[0:R, g, k * P:(k + 1) * P],
                                           pick[0:R, g, :], start=(g == 0), stop=(g == GROUPS - 1))
                    mm.then_inc(gather_done, 1)

            def slot_info(i, b):
                for s in range(2):
                    o = bank[5][:, 2 * CW + 4 * s:2 * CW + 4 * s + 4]
                    for g in range(GROUPS):
                        R = ROWS[g]
                        mm = pe.matmul(o, pick[0:R, g, s * TAIL:s * TAIL + P],
                                       info[0:R, bass.ds(2 * i + b, 1), g, :].rearrange("p o c -> p (o c)"),
                                       start=(g == 0), stop=(g == GROUPS - 1))
                mm.then_inc(slots_in_psum, 1)

            def gate_up(i, b):
                hi, lo = (w.rearrange("p (k f) -> p k f", k=KD) for w in (w_split[b][0][:, :], w_split[b][1][:, :]))
                pe.wait_ge(w12_hi_done, W12_PARTS * (2 * i + b + 1))
                for n in range(2):
                    pe.wait_ge(w12_lo_done[n], W12_PARTS // 2 * (2 * i + b + 1))
                for fc in range(FC):
                    pe.wait_ge(h_bank[fc % 4], 2 * (2 * i + b) + fc // 4 + 1)
                    for part, off in ((0, 0), (1, F)):
                        o = bank[fc % 4][:, part * CW:part * CW + CW]
                        ws = slice(off + fc * P, off + (fc + 1) * P)
                        for k in range(KD):
                            pe.matmul(o, hi[:, k, ws], xb[:, k, 0, :], start=(k == 0), stop=False)
                            pe.matmul(o, hi[:, k, ws], xb[:, k, 1, :], start=False, stop=False)
                            mm = pe.matmul(o, lo[:, k, ws], xb[:, k, 0, :], start=False, stop=(k == KD - 1))
                    mm.then_inc(gu_done, 1)

            def down(i, b):
                hi, lo = (w.rearrange("p (f d) -> p f d", f=FC) for w in (w_split[b][2][:, :], w_split[b][3][:, :]))
                pe.wait_ge(w3_hi_done, 2 * i + b + 1)
                pe.wait_ge(w3_lo_done, 2 * i + b + 1)
                for s in range(2):
                    pe.wait_ge(yw_done[s], 2 * i + b + 1)
                    o = bank[6 + s][:, 0:D]
                    slots = slice(s * TAIL, s * TAIL + P)
                    for fc in range(FC):
                        if s == 0:
                            pe.wait_ge(hid_hi_done, FC * (2 * i + b) + fc + 1)
                            pe.wait_ge(hid_lo_done, 4 + FC * (2 * i + b) + fc + 1)
                        pe.matmul(o, hid_hi[:, fc, slots], hi[:, fc, :], start=(fc == 0), stop=False)
                        pe.matmul(o, hid_hi[:, fc, slots], lo[:, fc, :], start=False, stop=False)
                        mm = pe.matmul(o, hid_lo[:, fc, slots], hi[:, fc, :], start=False, stop=(fc == FC - 1))
                    mm.then_inc(y_done, 1)

            def expert(i, b, last):
                pe.wait_ge(xb_done, 2 * (2 * i + b) + 2)
                slot_info(i, b)
                gate_up(i, b)
                if not last:
                    gather(i + b, 1 - b)
                down(i, b)

            pe.wait_ge(xn_hi_done, GROUPS)
            pe.wait_ge(xn_lo_done, GROUPS)
            gather(0, 0)
            pe.wait_ge(info_done, 1)
            with pe.Fori(0, PAIRS - 1) as i:
                expert(i, 0, False)
                expert(i, 1, False)
            expert(PAIRS - 1, 0, False)
            expert(PAIRS - 1, 1, True)

        @block.scalar
        def _(act):
            act.dma_start(wp_sb[:, :, :], wpT).then_inc(in_embed, 16)
            act.dma_start(ident[:, :], c_ident).then_inc(in_ident, 16)
            act.dma_start(w_sb[:, :, :, :], wqkvoT).then_inc(in_attn, 16)

            def copy_hnT(g):
                R = ROWS[g]
                act.wait_ge(hnT_in_psum, g + 1)
                act.activation(hnT[:, :, cols(g)], bank[2 + g % 2][:, 0:2 * P].rearrange("p (k c) -> p k c", k=KD)[:, :, 0:R],
                               ACT.Copy).then_inc(hnT_done, 1)

            def copy_v(g):
                R = ROWS[g]
                act.wait_ge(v_in_psum, g + 1)
                act.activation(v_sb[0:R, g, :], bank[4 + g % 2][0:R, 0:D], ACT.Copy).then_inc(v_done, 1)

            for t in range(GROUPS + 2):
                if 1 <= t <= GROUPS:
                    copy_hnT(t - 1)
                if t >= 2:
                    copy_v(t - 2)

            act.wait_ge(in_attn, 112)
            act.activation(gate[:, :], gate[:, :], ACT.Exp, scale=-1.0).then_inc(gate_exp, 1)
            QK_BANK = (0, 1, 6, 7)
            for n, (m, hf) in enumerate(WIDE):
                act.wait_ge(qk_in_psum, n + 1)
                act.activation(qT[:, m, half(hf)], bank[QK_BANK[n]][:, 0:HALF], ACT.Copy).then_inc(q_done, 1)
                act.wait_ge(qneg_done, n + 1)
                act.activation(qneg[:, m, half(hf)], qneg[:, m, half(hf)], ACT.Exp).then_inc(qexp_done, 1)
            for n, (m, hf) in enumerate(WIDE):
                act.wait_ge(qk_in_psum, 4 + n + 1)
                act.activation(kT[:, m, half(hf)], bank[QK_BANK[n]][:, 0:HALF], ACT.Copy).then_inc(k_done, 1)

            def split_w12(i, b, parts):
                for n in parts:
                    if n == 0:
                        act.wait_ge(w12_in[b], 16 * i + 16)
                    piece = slice(n * W12_PART, (n + 1) * W12_PART)
                    act.activation(w_split[b][0][:, piece], w12[b][:, piece], ACT.Copy).then_inc(w12_hi_done, 1)

            def softmax(t):
                R = ROWS[t]
                act.wait_ge(max_done, t + 1)
                if t >= 2:
                    act.wait_ge(pT_in_psum, t - 1)
                for hd in range(HEADS):
                    a = act.activation(probs[0:R, t % 2, hd, 0:R], bank[S_BANK[t % 2][hd % 2]][0:R, (hd // 2) * R:(hd // 2 + 1) * R], ACT.Exp,
                                       bias=negmax[0:R, t, hd:hd + 1], accum_out=psums[0:R, t, hd:hd + 1])
                a.then_inc(exp_done, 1)

            def copy_probsT(g):
                R = ROWS[g]
                act.wait_ge(pT_in_psum, g + 1)
                if g >= 2:
                    act.wait_ge(pv_done, g - 1)
                act.activation(probsT[0:R, g % 2, :, 0:R], bank[PT_BANK][0:R, 0:HEADS * R].rearrange("p (h c) -> p h c", h=HEADS),
                               ACT.Copy).then_inc(pT_done, 1)

            def split_xn(g):
                R = ROWS[g]
                act.wait_ge(xn_done, g + 1)
                act.activation(xn_hi[0:R, g, :], xn[0:R, g, :], ACT.Copy).then_inc(xn_hi_done, 1)

            def copy_xnT(g):
                R = ROWS[g]
                act.wait_ge(xnT_in_psum, g + 1)
                if g >= 2:
                    act.wait_ge(logits_in_psum, g - 1)
                act.activation(xnT[:, g % 2, :, 0:R], bank[ROUTER_BANK][:, 0:2 * P].rearrange("p (k c) -> p k c", k=KD)[:, :, 0:R],
                               ACT.Copy).then_inc(xnT_done, 1)

            softmax(0)
            act.wait_ge(denT_in_psum, 1)
            first = GROUPS // 2 * G_ROWS
            act.activation(denT[:, 0:first], bank[4][0:2 * HEADS, 0:first], ACT.Copy).then_inc(denT_done, 1)
            act.activation(denT[:, first:T], bank[5][0:2 * HEADS, 0:T - first], ACT.Copy).then_inc(denT_done, 1)
            for n in range(len(WIDE)):
                act.wait_ge(mem_in_psum, n + 1)
                if n >= 2:
                    act.wait_ge(mem_done, n - 1)
                act.activation(memgate[:, n % 2, :], bank[4 + n % 2][:, 0:HALF], ACT.Copy).then_inc(memgate_done, 1)
            split_w12(0, 0, (0,))
            for t in range(GROUPS + 7):
                for lag, stage in ((1, softmax), (6, split_xn), (5, copy_xnT), (2, copy_probsT)):
                    if 0 <= t - lag < GROUPS and not (stage == softmax and t == 1):
                        stage(t - lag)
                if 1 <= t < W12_PARTS:
                    split_w12(0, 0, (t,))
            act.wait_ge(gap_done, 1)
            act.activation(e1[:, :], gap[:, :], ACT.Exp).then_inc(e1_done, 1)

            def take_tokens(i, b):
                for k in range(KD):
                    act.wait_ge(gather_done, 2 * (2 * i + b) + k + 1)
                    act.activation(xb[:, k, :, :], bank[4 + k][:, 0:2 * CW].rearrange("p (b c) -> p b c", b=2),
                                   ACT.Copy).then_inc(xb_done, 1)

            def expert(i, b, last):
                for fc in range(FC + 1):
                    if fc < FC:
                        act.wait_ge(gu_done, FC * (2 * i + b) + fc + 1)
                        act.activation(sg[:, fc % 4, :], bank[fc % 4][:, 0:CW], ACT.Silu).then_inc(silu_done, 1)
                    if fc >= 1:
                        n = fc - 1
                        act.wait_ge(h_bank[n % 4], 2 * (2 * i + b) + n // 4 + 2)
                        act.activation(hid_hi[:, n, :], hid[:, n % 4, :], ACT.Copy).then_inc(hid_hi_done, 1)
                    if fc % 2 == 0 and fc < FC and not last:
                        split_w12(i + b, 1 - b, (fc // 2,))
                if not last:
                    take_tokens(i + b, 1 - b)
                act.wait_ge(slots_done, 2 * i + b + 1)
                for s in range(2):
                    act.wait_ge(y_done, 2 * (2 * i + b) + s + 1)
                    act.wait_ge(yw_free[2 * b + s], i + 1)
                    act.activation(yw[2 * b + s][:, :], bank[6 + s][:, 0:D], ACT.Copy,
                                   scale=w_slot[:, s:s + 1]).then_inc(yw_done[s], 1)

            take_tokens(0, 0)
            with act.Fori(0, PAIRS - 1) as i:
                expert(i, 0, False)
                expert(i, 1, False)
            expert(PAIRS - 1, 0, False)
            expert(PAIRS - 1, 1, True)

        @block.vector
        def _(dve):
            steps = [0]

            def then(ins):
                steps[0] += 1
                ins.then_inc(dve_step, 1)
                dve.wait_ge(dve_step, steps[0])

            dve.memset(minus_half[:, :], -0.5).then_inc(consts_set, 1)
            dve.memset(ones[:, :], 1.0)
            dve.wait_ge(in_ident, 16)
            dve.tensor_copy(ident_bf[:, :], ident[0:G_ROWS, 0:G_ROWS])
            dve.memset(logits[:, :, :], 0.0)
            dve.memset(top[:, :, :], 0.0)
            dve.memset(top_i[:, :, :], 0)
            dve.memset(den[:, :, :], 1.0)
            then(dve.memset(info[:, :, :, :].bitcast(F32), 0.0))

            def norm1(g):
                R = ROWS[g]
                dve.wait_ge(rstd1_done, g + 1)
                dve.tensor_scalar(hn[0:R, g, :], h[0:R, g, :], mv1[0:R, g, 0:1], rstd1[0:R, g:g + 1],
                                  ALU.subtract, ALU.mult).then_inc(hn_done, 1)

            for g in range(GROUPS):
                R = ROWS[g]
                dve.wait_ge(embed_done, g + 1)
                if g == 0:
                    dve.wait_ge(pos_done, 1)
                dve.tensor_tensor(h[0:R, g, :], bank[g % 2][0:R, 0:D], pos[0:R, :], ALU.add).then_inc(h_copied, 1)
                dve.wait_ge(h_copied, g + 1)
                then(dve.bn_stats(stats[0:R, g, :], h[0:R, g, :]))
                then(dve.bn_aggr(mv1[0:R, g, :], stats[0:R, g, :]))
                dve.tensor_scalar(var1[0:R, g:g + 1], mv1[0:R, g, 1:2], EPS, None, ALU.add).then_inc(var1_done, 1)
                norm1(g)

            dve.wait_ge(in_attn, 112)
            dve.tensor_copy(head_rows_r[:, :, :], head_rows[:, :, :])
            dve.tensor_copy(mask_bf[:, :], mask[:, :]).then_inc(mask_set, 1)
            dve.wait_ge(gate_exp, 1)
            then(dve.tensor_scalar(gate[:, :], gate[:, :], 1.0, None, ALU.add))
            then(dve.reciprocal(gate[:, :], gate[:, :]))
            then(dve.tensor_scalar(keep[:, :], gate[:, :], -1.0, 1.0, ALU.mult, ALU.add))

            for n, (m, hf) in enumerate(WIDE):
                dve.wait_ge(q_done, n + 1)
                dve.tensor_scalar(qneg[:, m, half(hf)], qT[:, m, half(hf)], 0.0, None, ALU.min).then_inc(qneg_done, 1)
            for n, (m, hf) in enumerate(WIDE):
                dve.wait_ge(qexp_done, n + 1)
                dve.scalar_tensor_tensor(out=sqT[:, m, half(hf)], in0=qT[:, m, half(hf)], scalar=0.0,
                                         in1=qneg[:, m, half(hf)], op0=ALU.max, op1=ALU.add).then_inc(sq_done, 1)

            def row_max(g):
                R = ROWS[g]
                dve.wait_ge(s_in_psum, g + 1)
                for hh in range(2):
                    max_ins = dve.tensor_reduce(negmax[0:R, g, hh::2], bank[S_BANK[g % 2][hh]][0:R, 0:2 * R].rearrange("p (h c) -> p h c", h=2),
                                                AX_X, ALU.max)
                then(max_ins)
                dve.tensor_scalar(negmax[0:R, g, :], negmax[0:R, g, :], -1.0, None, ALU.mult).then_inc(max_done, 1)

            def memory_den():
                dve.wait_ge(den_in_psum, 1)
                full = (GROUPS - 1) * HEADS
                den2 = den[:, :, :].rearrange("p g h -> p (g h)")
                dve.tensor_scalar(den2[:, 0:full], bank[4][0:G_ROWS, 0:full], 1e-6, None, ALU.add)
                then(dve.tensor_scalar(den2[0:ROWS[-1], full:full + HEADS], bank[4][0:ROWS[-1], full:full + HEADS], 1e-6, None, ALU.add))
                then(dve.reciprocal(den2, den2))
                then(dve.tensor_tensor(den[:, :, :], den[:, :, :], gate[:, :].unsqueeze(1).broadcast_to([G_ROWS, GROUPS, HEADS]), ALU.mult))
                then(dve.tensor_copy(den_split[:, :, 0, :], den[:, :, :]))
                dve.tensor_tensor(den_split[:, :, 1, :], den[:, :, :], den_split[:, :, 0, :].bitcast(F32),
                                  ALU.subtract).then_inc(den_done, 1)

            def memory_part(n, m, hf):
                dve.wait_ge(memgate_done, n + 1)
                dve.tensor_tensor(memT[:, m, half(hf)], bank[6 + n % 2][:, 0:HALF], memgate[:, n % 2, :], ALU.mult).then_inc(mem_done, 1)

            def normalise(g):
                R = ROWS[g]
                dve.wait_ge(exp_done, g + 1)
                then(dve.reciprocal(psums[0:R, g, :], psums[0:R, g, :]))
                then(dve.tensor_tensor(psums[0:R, g, :], psums[0:R, g, :], keep[0:R, :], ALU.mult))
                dve.tensor_tensor(probs[0:R, g % 2, :, 0:R], probs[0:R, g % 2, :, 0:R],
                                  psums[0:R, g, :].unsqueeze(2).broadcast_to([R, HEADS, R]), ALU.mult).then_inc(pn_done, 1)

            def add_memory(g):
                R = ROWS[g]
                dve.wait_ge(pv_done, g + 1)
                if g == 0:
                    dve.wait_ge(mem_done, 4)
                if g >= 2:
                    dve.wait_ge(wo_done, g - 1)
                dve.tensor_tensor(aoT[:, g % 2, :, 0:R], bank[PV_BANK][:, 0:2 * R].rearrange("p (m c) -> p m c", m=2),
                                  memT[:, :, cols(g)], ALU.add).then_inc(ao_done, 1)

            def residual(g):
                R = ROWS[g]
                dve.wait_ge(wo_done, g + 1)
                dve.wait_ge(h_bo_done, g + 1)
                dve.tensor_tensor(h2[0:R, g, :], bank[WO_BANK][0:R, 0:D], h[0:R, g, :], ALU.add).then_inc(h2_done, 1)
                dve.wait_ge(h2_done, g + 1)
                then(dve.bn_stats(stats[0:R, g, :], h2[0:R, g, :]))
                then(dve.bn_aggr(mv2[0:R, g, :], stats[0:R, g, :]))
                dve.tensor_scalar(var2[0:R, g:g + 1], mv2[0:R, g, 1:2], 1.0 + EPS, EPS * EPS, ALU.mult, ALU.add).then_inc(var2_done, 1)

            def norm2(g):
                R = ROWS[g]
                if g == 0:
                    dve.wait_ge(in_ffn, 128)
                then(dve.scalar_tensor_tensor(out=xg[0:R, g, :], in0=h2[0:R, g, :], scalar=mv2[0:R, g, 0:1],
                                              in1=gamma_b[0:R, :], op0=ALU.subtract, op1=ALU.mult))
                dve.wait_ge(rstd2_done, g + 1)
                dve.scalar_tensor_tensor(out=xn[0:R, g, :], in0=xg[0:R, g, :], scalar=rstd2[0:R, g:g + 1],
                                         in1=beta_b[0:R, :], op0=ALU.mult, op1=ALU.add).then_inc(xn_done, 1)

            def rank(g):
                R = ROWS[g]
                dve.wait_ge(logits_in_psum, g + 1)
                dve.tensor_scalar(logits[0:R, g, :], bank[ROUTER_BANK][0:R, 2 * P:2 * P + EXPERTS], 1e4, -1e4,
                                  ALU.min, ALU.max).then_inc(logits_read, 1)
                dve.wait_ge(logits_read, g + 1)
                then(dve.max(top[0:R, g, :], logits[0:R, g, :]))
                then(dve.max_index(top_i[0:R, g, :], top[0:R, g, :], logits[0:R, g, :]))

            def split_w12(i, b):
                for n in range(W12_PARTS // 2):
                    dve.wait_ge(w12_hi_done, W12_PARTS * (2 * i + b) + n + 1)
                    piece = slice(n * W12_PART, (n + 1) * W12_PART)
                    yield dve.tensor_tensor(w_split[b][1][:, piece], w12[b][:, piece], w_split[b][0][:, piece].bitcast(F32),
                                            ALU.subtract).then_inc(w12_lo_done[0], 1)

            def split_w3(i, b):
                dve.wait_ge(w3_in[b], 16 * i + 16)
                dve.tensor_copy(w_split[b][2][:, :], w3[b][:, :]).then_inc(w3_hi_done, 1)

            def choose(i, b):
                dve.tensor_tensor(pick[:, :, :], slot_iota[:, :].unsqueeze(1).broadcast_to([G_ROWS, GROUPS, CW]),
                                  place[:, bass.ds(2 * i + b, 1), :].rearrange("p o g -> p (o g)").unsqueeze(2).broadcast_to([G_ROWS, GROUPS, CW]),
                                  ALU.is_equal).then_inc(pick_done, 1)

            memory_den()
            row_max(0)
            row_max(1)
            for n, (m, hf) in enumerate(WIDE):
                memory_part(n, m, hf)
            first_w12 = split_w12(0, 0)
            for t in range(GROUPS + 7):
                for lag, stage in ((2, normalise), (5, residual), (6, rank), (0, row_max), (5, norm2), (3, add_memory)):
                    if 0 <= t - lag < GROUPS and not (stage == row_max and t < 2):
                        stage(t - lag)
                if t in (2, 3):
                    next(first_w12)
                if t == 4:
                    split_w3(0, 0)
            dve.tensor_tensor(gap[:, :], top[:, :, 1], top[:, :, 0], ALU.subtract).then_inc(gap_done, 1)
            then(dve.tensor_copy(top_f[:, :, :], top_i[:, :, :]))
            hots = expert_iota[:, :].unsqueeze(1).broadcast_to([G_ROWS, GROUPS, EXPERTS])
            dve.tensor_tensor(hot0[:, :, :], hots, top_f[:, :, 0:1].broadcast_to([G_ROWS, GROUPS, EXPERTS]), ALU.is_equal)
            then(dve.tensor_tensor(hot1[:, :, :], hots, top_f[:, :, 1:2].broadcast_to([G_ROWS, GROUPS, EXPERTS]), ALU.is_equal))
            R = ROWS[-1]
            then(dve.memset(hot[:, GROUPS - 1, :], 0.0))
            dve.tensor_tensor(hot[0:R, GROUPS - 1, :], hot0[0:R, GROUPS - 1, :], hot1[0:R, GROUPS - 1, :], ALU.add)
            dve.tensor_tensor(hot[:, 0:GROUPS - 1, :], hot0[:, 0:GROUPS - 1, :], hot1[:, 0:GROUPS - 1, :], ALU.add).then_inc(hot_done, 1)
            dve.wait_ge(count_done, 1)
            place_gp = place[:, :, :].rearrange("p e g -> p g e")
            then(dve.scalar_tensor_tensor(out=place_gp, in0=bank[PLACE_BANK][0:G_ROWS, 0:GROUPS * EXPERTS].rearrange("p (g e) -> p g e", e=EXPERTS),
                                          scalar=1.0, in1=hot[:, :, :], op0=ALU.add, op1=ALU.mult))
            dve.tensor_scalar(place[:, :, :], place[:, :, :], -1.0, None, ALU.add).then_inc(place_done, 1)
            dve.wait_ge(place_done, 1)
            dve.wait_ge(xn_lo_done, GROUPS)
            choose(0, 0)
            dve.wait_ge(e1_done, 1)
            then(dve.tensor_scalar(p0[:, :], e1[:, :], 1.0, 1e-12, ALU.add, ALU.add))
            then(dve.reciprocal(p0[:, :], p0[:, :]))
            then(dve.tensor_tensor(p1[:, :], p0[:, :], e1[:, :], ALU.mult))
            wt_gp = wt[:, :, :].rearrange("p e g -> p g e")
            wt1_gp = wt1[:, :, :].rearrange("p e g -> p g e")
            dve.tensor_tensor(wt_gp, hot0[:, :, :], p0[:, :].unsqueeze(2).broadcast_to([G_ROWS, GROUPS, EXPERTS]), ALU.mult)
            then(dve.tensor_tensor(wt1_gp, hot1[:, :, :], p1[:, :].unsqueeze(2).broadcast_to([G_ROWS, GROUPS, EXPERTS]), ALU.mult))
            then(dve.tensor_tensor(wt[:, :, :], wt[:, :, :], wt1[:, :, :], ALU.add))
            dve.tensor_copy(info[:, :, :, 0], token_plus1[:, :].unsqueeze(1).broadcast_to([G_ROWS, EXPERTS, GROUPS]))
            then(dve.tensor_copy(info[:, :, :, 1], wt[:, :, :]))
            dve.tensor_tensor(info[:, :, :, 2], wt[:, :, :], info[:, :, :, 1].bitcast(F32), ALU.subtract).then_inc(info_done, 1)

            def slots(i, b):
                step = 4 * (2 * i + b)
                dve.wait_ge(slots_in_psum, 2 * i + b + 1)
                dve.wait_ge(yw_free[2 * b + 1], i + 1)
                o = bank[5][:, 2 * CW:2 * CW + 8].rearrange("p (n c) -> p n c", c=4)
                dve.tensor_copy(slot_row[:, :], o[:, :, 0])
                dve.tensor_copy(w_slot[:, :], o[:, :, 1]).then_inc(slots_stage, 1)
                dve.wait_ge(slots_stage, step + 1)
                dve.tensor_scalar(slot_far[:, :], slot_row[:, :], 0.0, FAR, ALU.is_equal, ALU.mult)
                dve.tensor_tensor(w_slot[:, :], w_slot[:, :], o[:, :, 2], ALU.add).then_inc(slots_stage, 1)
                dve.wait_ge(slots_stage, step + 2)
                dve.scalar_tensor_tensor(out=slot_row[:, :], in0=slot_row[:, :], scalar=-1.0, in1=slot_far[:, :],
                                         op0=ALU.add, op1=ALU.add).then_inc(slots_stage, 1)
                dve.wait_ge(slots_stage, step + 3)
                dve.tensor_tensor(slot_row[:, :], slot_row[:, :], dup_far[:, :], ALU.add).then_inc(slots_stage, 1)
                dve.wait_ge(slots_stage, step + 4)
                dve.tensor_copy(slot_token[b][:, :], slot_row[:, :]).then_inc(slots_done, 1)

            def expert(i, b, last):
                pieces = None if last else split_w12(i + b, 1 - b)
                for fc in range(FC + 2):
                    if fc < FC:
                        dve.wait_ge(hid_lo_done, FC * (2 * i + b) + fc + 1)
                        dve.wait_ge(silu_done, FC * (2 * i + b) + fc + 1)
                        dve.tensor_tensor(hid[:, fc % 4, :], sg[:, fc % 4, :], bank[fc % 4][:, CW:2 * CW],
                                          ALU.mult).then_inc(h_bank[fc % 4], 1)
                    if fc >= 2:
                        n = fc - 2
                        dve.wait_ge(hid_hi_done, FC * (2 * i + b) + n + 1)
                        dve.tensor_tensor(hid_lo[:, n, :], hid[:, n % 4, :], hid_hi[:, n, :].bitcast(F32),
                                          ALU.subtract).then_inc(hid_lo_done, 1)
                    if fc == 0:
                        slots(i, b)
                    if not last:
                        if fc == 2:
                            choose(i + b, 1 - b)
                        if fc in (3, 5):
                            next(pieces)
                        if fc == 7:
                            split_w3(i + b, 1 - b)

            with dve.Fori(0, PAIRS - 1) as i:
                expert(i, 0, False)
                expert(i, 1, False)
            expert(PAIRS - 1, 0, False)
            expert(PAIRS - 1, 1, True)

        @block.gpsimd
        def _(pool):
            pool.wait_ge(in_pos, 32)
            pool.tensor_tensor(pos[:, :], pos[:, :], bias[:, :], ALU.add).then_inc(pos_done, 1)
            pool.wait_ge(consts_set, 1)
            for g in range(GROUPS):
                R = ROWS[g]
                pool.wait_ge(var1_done, g + 1)
                pool.tensor_tensor(rstd1[0:R, g:g + 1], var1[0:R, g:g + 1], minus_half[0:R, :], ALU.pow).then_inc(rstd1_done, 1)
            pool.wait_ge(in_attn, 112)
            for g in range(GROUPS):
                R = ROWS[g]
                pool.wait_ge(hn_done, g + 1)
                pool.tensor_tensor(h[0:R, g, :], h[0:R, g, :], bo_b[0:R, :], ALU.add).then_inc(h_bo_done, 1)

            def split(i, b):
                for n in range(W12_PARTS // 2, W12_PARTS):
                    pool.wait_ge(w12_hi_done, W12_PARTS * (2 * i + b) + n + 1)
                    piece = slice(n * W12_PART, (n + 1) * W12_PART)
                    pool.tensor_tensor(w_split[b][1][:, piece], w12[b][:, piece], w_split[b][0][:, piece].bitcast(F32),
                                       ALU.subtract).then_inc(w12_lo_done[1], 1)
                pool.wait_ge(w3_hi_done, 2 * i + b + 1)
                pool.tensor_tensor(w_split[b][3][:, :], w3[b][:, :], w_split[b][2][:, :].bitcast(F32),
                                   ALU.subtract).then_inc(w3_lo_done, 1)

            def split_xn(g):
                R = ROWS[g]
                pool.wait_ge(xn_hi_done, g + 1)
                pool.tensor_tensor(xn_lo[0:R, g, :], xn[0:R, g, :], xn_hi[0:R, g, :].bitcast(F32), ALU.subtract).then_inc(xn_lo_done, 1)

            for t in range(GROUPS + 1):
                if t < GROUPS:
                    R = ROWS[t]
                    pool.wait_ge(var2_done, t + 1)
                    pool.tensor_tensor(rstd2[0:R, t:t + 1], var2[0:R, t:t + 1], minus_half[0:R, :], ALU.pow).then_inc(rstd2_done, 1)
                if t >= 1:
                    split_xn(t - 1)
                if t == 2:
                    split(0, 0)

            def scatter(e, s):
                n = 2 * (e % 2) + s
                pool.wait_ge(yw_done[s], e + 2)
                pool.indirect_dma_start(out=out, out_offset=bass.IndirectOffsetOnAxis(ap=slot_token[e % 2][:, s:s + 1], axis=0),
                                        in_=yw[n][:, :], in_offset=None, bounds_check=T - 1, oob_is_err=False,
                                        compute_op=ALU.add).then_inc(scattered[n], 16)
                pool.wait_ge(scattered[n], 16 * (e // 2) + 16)
                pool.sem_inc(yw_free[n], 1)

            pool.wait_ge(h2_stored, 16 * GROUPS)
            for e in range(EXPERTS):
                if e + 1 < EXPERTS:
                    split((e + 1) // 2, (e + 1) % 2)
                for s in range(2):
                    scatter(e, s)


def _constants():
    q = np.arange(G_ROWS)
    seen = (q[:, None] // S == q[None, :] // S) & (q[:, None] >= q[None, :])
    mask = np.where(seen, 0, MASKED).astype(np.float32)
    before = (q[:, None] < q[None, :]).astype(np.float32)
    slots = np.arange(CW, dtype=np.float32)
    slots[CAP:] = -2 - np.arange(CW - CAP)
    token = np.minimum(q[:, None] + G_ROWS * np.arange(GROUPS)[None, :] + 1, T).astype(np.float32)
    dup = np.zeros((P, 2), np.float32)
    dup[:P - TAIL, 1] = FAR
    head = np.zeros((2, HEADS, 2, P), np.float32)
    for n in range(HEADS):
        head[:, n, n // 2, n % 2 * HD:(n % 2 + 1) * HD] = 1
    return [mask, before, np.eye(P, dtype=np.float32), slots, token, dup, head.reshape(2 * HEADS, 2, P)]


def kernel(x, cls_tok, L0_tok_W_proj, L0_tok_b_proj, L0_tok_pos_emb, L0_attn_Wq, L0_attn_Wk, L0_attn_Wv, L0_attn_Wo,
           L0_attn_bo, L0_attn_betas, L0_attn_mem, L0_attn_z, L0_ffn_ln_gamma, L0_ffn_ln_beta, L0_ffn_router_w,
           L0_ffn_w12, L0_ffn_w3):
    import concourse.bacc as bacc
    from concourse.bass_utils import run_bass_kernel_spmd

    side = SIDE // PATCH

    def to_partitions(a, k):
        return a.reshape(k, P, -1).transpose(1, 0, 2)

    patches = np.asarray(x).reshape(IMAGES, side, PATCH, side, PATCH, CHANNELS).transpose(0, 1, 3, 2, 4, 5).reshape(IMAGES, NPATCH, -1)
    tokens = np.pad(patches, ((0, 0), (1, 0), (0, 0))).reshape(T, -1)
    tokens = np.pad(tokens, ((0, GROUPS * G_ROWS - T), (0, 0))).reshape(GROUPS, G_ROWS, KE, P)
    image_rows = np.concatenate([np.asarray(cls_tok)[0], np.asarray(L0_tok_pos_emb)])
    bias_rows = np.zeros_like(image_rows)
    bias_rows[1:] = np.asarray(L0_tok_b_proj)
    mem, z = np.asarray(L0_attn_mem), np.asarray(L0_attn_z)
    mem_diag = np.zeros((P, 2, P), mem.dtype)
    z4 = np.zeros((P, 2, HEADS), z.dtype)
    for n in range(HEADS):
        rows = slice(n % 2 * HD, (n % 2 + 1) * HD)
        mem_diag[rows, n // 2, rows] = mem[n]
        z4[rows, n // 2, n] = z[n, :, 0]
    weights = [np.asarray(w).T for w in (L0_attn_Wq, L0_attn_Wk, L0_attn_Wv, L0_attn_Wo)]
    arrays = [
        tokens.transpose(0, 3, 2, 1),
        to_partitions(np.asarray(L0_tok_W_proj).T, KE),
        np.tile(image_rows, (IMG_PER_GROUP, 1)),
        np.tile(bias_rows, (IMG_PER_GROUP, 1)),
        np.stack([to_partitions(w, KD) for w in weights], axis=1),
        np.asarray(L0_attn_bo), np.asarray(L0_attn_betas).reshape(HEADS), mem_diag, z4,
        np.asarray(L0_ffn_ln_gamma), np.asarray(L0_ffn_ln_beta),
        to_partitions(np.asarray(L0_ffn_router_w).T, KD),
        np.asarray(L0_ffn_w12).transpose(0, 2, 1).reshape(EXPERTS, KD, P, 2 * F).transpose(0, 2, 1, 3).reshape(EXPERTS, P, -1),
        np.asarray(L0_ffn_w3).transpose(0, 2, 1).reshape(EXPERTS, FC, P, D).transpose(0, 2, 1, 3).reshape(EXPERTS, P, -1),
    ] + _constants()

    nc = bacc.Bacc("TRN2", target_bir_lowering=False, num_devices=1)
    inputs, args = {}, []
    for n, a in enumerate(arrays):
        a = np.ascontiguousarray(a)
        inputs[f"in{n}"] = a
        args.append(nc.dram_tensor(f"in{n}", a.shape, mybir.dt.from_np(a.dtype), kind="ExternalInput").ap())
    args.append(nc.dram_tensor("out", (T, D), F32, kind="ExternalOutput").ap())
    vit_tower(nc, *args)
    r = run_bass_kernel_spmd(nc, [inputs], core_ids=[0])
    return r.results[0]["out"].reshape(IMAGES, S, D)
```

```python
from contextlib import ExitStack

import numpy as np
import concourse.bass as bass
from concourse import mybir

F32 = mybir.dt.float32
F32R = mybir.dt.float32r
BF16 = mybir.dt.bfloat16
U32 = mybir.dt.uint32
ALU = mybir.AluOpType
ACT = mybir.ActivationFunctionType
AX_X = mybir.AxisListType.X

P = 128
D = 256
KD = D // P
IMAGES, SIDE, PATCH, CHANNELS = 16, 96, 16, 3
NPATCH = (SIDE // PATCH) ** 2
S = NPATCH + 1
T = IMAGES * S
KE = PATCH * PATCH * CHANNELS // P
IMG_PER_GROUP = P // S
G_ROWS = IMG_PER_GROUP * S
GROUPS = -(-T // G_ROWS)
ROWS = [min(G_ROWS, T - g * G_ROWS) for g in range(GROUPS)]
HEADS, HD = 4, 64
HALF = T // 2
EXPERTS, TOPK = 8, 2
F = 1024
FC = F // P
CAP = -(-T * TOPK * 5 // (4 * EXPERTS))
CW = 192
TAIL = CW - P
PAIRS = EXPERTS // 2
EPS = 1e-5
W12_PARTS = 4
W12_PART = KD * 2 * F // W12_PARTS
FAR = 4096.0
MASKED = -3.0e38


def vit_tower(nc, xT, wpT, pos_cls, bias_rows, wqkvoT, bo, betas, mem_diag, z4, gamma, beta, routerT, w12T, w3T,
              c_mask, c_before, c_ident, c_slots, c_token, c_dup, c_head, out):
    with ExitStack() as ctx:
        def sb(name, shape, dt=F32):
            return ctx.enter_context(nc.sbuf_tensor(name, shape, dt))

        def sem(name):
            return ctx.enter_context(nc.semaphore(name))

        bank = [ctx.enter_context(nc.psum_tensor(f"bank{i}", [P, 512], F32)) for i in range(8)]

        slot_iota = sb("slot_iota", [G_ROWS, CW])
        expert_iota = sb("expert_iota", [G_ROWS, EXPERTS])
        token_plus1 = sb("token_plus1", [G_ROWS, GROUPS])
        dup_far = sb("dup_far", [P, 2])
        h2 = sb("h2", [P, GROUPS, D])
        xn_hi = sb("xn_hi", [G_ROWS, GROUPS, D], F32R)
        xn_lo = sb("xn_lo", [G_ROWS, GROUPS, D], F32R)
        logits = sb("logits", [G_ROWS, GROUPS, EXPERTS])
        top = sb("top", [G_ROWS, GROUPS, 8])
        top_i = sb("top_i", [G_ROWS, GROUPS, 8], U32)
        top_f = sb("top_f", [G_ROWS, GROUPS, 8])
        hot0 = sb("hot0", [G_ROWS, GROUPS, EXPERTS])
        hot1 = sb("hot1", [G_ROWS, GROUPS, EXPERTS])
        hot = sb("hot", [G_ROWS, GROUPS, EXPERTS])
        place = sb("place", [G_ROWS, EXPERTS, GROUPS])
        gap = sb("gap", [G_ROWS, GROUPS])
        e1 = sb("e1", [G_ROWS, GROUPS])
        p0 = sb("p0", [G_ROWS, GROUPS])
        p1 = sb("p1", [G_ROWS, GROUPS])
        wt = sb("wt", [G_ROWS, EXPERTS, GROUPS])
        wt1 = sb("wt1", [G_ROWS, EXPERTS, GROUPS])
        info = sb("info", [G_ROWS, EXPERTS, GROUPS, 4], F32R)
        w12 = [sb(f"w12_{b}", [P, KD * 2 * F]) for b in range(2)]
        w3 = [sb(f"w3_{b}", [P, FC * D]) for b in range(2)]

        def split_buffers(b):
            return [sb(f"{n}_{b}", [P, size], F32R) for n, size in
                    (("w12_hi", KD * 2 * F), ("w12_lo", KD * 2 * F), ("w3_hi", FC * D), ("w3_lo", FC * D))]

        w_split = [split_buffers(0)]

        dense = ExitStack()

        def sb1(name, shape, dt=F32):
            return dense.enter_context(nc.sbuf_tensor(name, shape, dt))

        ident = sb1("ident", [P, P])
        pos = sb1("pos", [G_ROWS, D])
        bias = sb1("bias", [G_ROWS, D])
        ident_bf = sb1("ident_bf", [G_ROWS, G_ROWS], BF16)
        mask_bf = sb1("mask_bf", [G_ROWS, G_ROWS], BF16)
        mask = sb1("mask", [G_ROWS, G_ROWS])
        before = sb1("before", [G_ROWS, G_ROWS])
        ones = sb1("ones", [G_ROWS, G_ROWS])
        x_flat = sb1("x_flat", [P, GROUPS * KE * G_ROWS])
        x_sb = x_flat[:, :].rearrange("p (g k c) -> p g k c", g=GROUPS, k=KE)
        x_taken = [0]

        def in_x_space(rows, a, b, c):
            start = x_taken[0]
            x_taken[0] += a * b * c
            return x_flat[0:rows, start:start + a * b * c].rearrange("p (a b c) -> p a b c", a=a, b=b)

        wp_sb = sb1("wp_sb", [P, KE, D])
        w_sb = sb1("w_sb", [P, 4, KD, D])
        bo_b = sb1("bo_b", [G_ROWS, D])
        gamma_b = sb1("gamma_b", [G_ROWS, D])
        beta_b = sb1("beta_b", [G_ROWS, D])
        router_sb = sb1("router_sb", [P, KD, EXPERTS])
        mem_bd = sb1("mem_bd", [P, 2, P])
        z_sb = sb1("z_sb", [P, 2, HEADS])
        head_rows = sb1("head_rows", [2 * HEADS, 2, P])
        head_rows_r = sb1("head_rows_r", [2 * HEADS, 2, P], F32R)
        gate = sb1("gate", [G_ROWS, HEADS])
        keep = sb1("keep", [G_ROWS, HEADS])
        h = sb1("h", [G_ROWS, GROUPS, D])
        hn = sb1("hn", [G_ROWS, GROUPS, D])
        hnT = sb1("hnT", [P, KD, T])
        v_sb = sb1("v_sb", [G_ROWS, GROUPS, D])
        qT = sb1("qT", [P, 2, T])
        kT = sb1("kT", [P, 2, T])
        qneg = sb1("qneg", [P, 2, T])
        sqT = sb1("sqT", [P, 2, T])
        memT = qneg
        den = sb1("den", [G_ROWS, GROUPS, HEADS])
        den_split = sb1("den_split", [G_ROWS, GROUPS, 2, HEADS], F32R)
        denT = sb1("denT", [2 * HEADS, T], F32R)
        memgate = in_x_space(P, 1, 2, HALF)[:, 0]
        probs = in_x_space(G_ROWS, 2, HEADS, G_ROWS)
        probsT = in_x_space(G_ROWS, 2, HEADS, G_ROWS)
        negmax = sb1("negmax", [G_ROWS, GROUPS, HEADS])
        psums = sb1("psums", [G_ROWS, GROUPS, HEADS])
        aoT = in_x_space(P, 2, 2, G_ROWS)
        xg = hn
        xn = hn
        xnT = sb1("xnT", [P, 2, KD, G_ROWS])
        stats = sb1("stats", [G_ROWS, GROUPS, 6])
        mv1 = sb1("mv1", [G_ROWS, GROUPS, 2])
        mv2 = sb1("mv2", [G_ROWS, GROUPS, 2])
        var1 = sb1("var1", [G_ROWS, GROUPS])
        var2 = sb1("var2", [G_ROWS, GROUPS])
        rstd1 = sb1("rstd1", [G_ROWS, GROUPS])
        rstd2 = sb1("rstd2", [G_ROWS, GROUPS])
        minus_half = sb1("minus_half", [G_ROWS, 1])
        dense.close()

        w_split.append(split_buffers(1))
        pick = sb("pick", [G_ROWS, GROUPS, CW], F32R)
        xb = sb("xb", [P, KD, 2, CW], F32R)
        hi_lo = sb("hi_lo", [P, 2, CW])
        gate_sum = sb("gate_sum", [P, 2, CW])
        up_sum = sb("up_sum", [P, 4, CW])
        sg = sb("sg", [P, 2, CW])
        hid = sb("hid", [P, 4, CW])
        hid_hi = [sb(f"hid_hi{b}", [P, FC, CW], F32R) for b in range(2)]
        hid_lo = [sb(f"hid_lo{b}", [P, FC, CW], F32R) for b in range(2)]
        slot_raw = sb("slot_raw", [P, 2, 4])
        slot_row = sb("slot_row", [P, 2])
        slot_far = sb("slot_far", [P, 2])
        w_slot = [sb(f"w_slot{b}", [P, 2]) for b in range(2)]
        slot_token = [sb(f"slot_token{b}", [P, 2], U32) for b in range(2)]
        yw = [h2[:, n, :] for n in range(4)]

        in_embed = sem("in_embed")
        in_x = [sem(f"in_x{g}") for g in range(GROUPS)]
        in_ident = sem("in_ident")
        in_pos = sem("in_pos")
        pos_done = sem("pos_done")
        in_attn = sem("in_attn")
        in_ffn = sem("in_ffn")
        consts_set = sem("consts_set")
        embed_done = sem("embed_done")
        h_copied = sem("h_copied")
        h_bo_done = sem("h_bo_done")
        var1_done = sem("var1_done")
        rstd1_done = sem("rstd1_done")
        hn_done = sem("hn_done")
        hnT_in_psum = sem("hnT_in_psum")
        hnT_done = sem("hnT_done")
        v_in_psum = sem("v_in_psum")
        v_done = sem("v_done")
        qk_in_psum = sem("qk_in_psum")
        q_done = sem("q_done")
        k_done = sem("k_done")
        qneg_done = sem("qneg_done")
        qexp_done = sem("qexp_done")
        sq_done = sem("sq_done")
        gate_exp = sem("gate_exp")
        gate_done = sem("gate_done")
        den_in_psum = sem("den_in_psum")
        den_done = sem("den_done")
        denT_in_psum = sem("denT_in_psum")
        denT_done = sem("denT_done")
        mem_in_psum = sem("mem_in_psum")
        memgate_done = sem("memgate_done")
        mem_done = sem("mem_done")
        s_in_psum = sem("s_in_psum")
        mask_set = sem("mask_set")
        max_done = sem("max_done")
        exp_done = sem("exp_done")
        pn_done = sem("pn_done")
        pT_in_psum = sem("pT_in_psum")
        pT_done = sem("pT_done")
        pv_done = sem("pv_done")
        ao_done = sem("ao_done")
        wo_done = sem("wo_done")
        h2_done = sem("h2_done")
        h2_stored = sem("h2_stored")
        var2_done = sem("var2_done")
        rstd2_done = sem("rstd2_done")
        xn_done = sem("xn_done")
        xn_hi_done = sem("xn_hi_done")
        xn_lo_done = sem("xn_lo_done")
        xnT_in_psum = sem("xnT_in_psum")
        xnT_done = sem("xnT_done")
        logits_in_psum = sem("logits_in_psum")
        logits_read = sem("logits_read")
        hot_done = sem("hot_done")
        count_done = sem("count_done")
        place_done = sem("place_done")
        gap_done = sem("gap_done")
        e1_done = sem("e1_done")
        info_done = sem("info_done")
        dve_step = sem("dve_step")
        w12_in = [sem(f"w12_in{b}") for b in range(2)]
        w3_in = [sem(f"w3_in{b}") for b in range(2)]
        pick_done = sem("pick_done")
        gather_done = sem("gather_done")
        xb_done = sem("xb_done")
        slots_in_psum = sem("slots_in_psum")
        slots_stage = sem("slots_stage")
        slots_done = sem("slots_done")
        gu_done = sem("gu_done")
        hi_lo_out = sem("hi_lo_out")
        silu_done = sem("silu_done")
        w12_hi_done = sem("w12_hi_done")
        w12_lo_done = [sem(f"w12_lo_done_{who}") for who in ("dve", "pool")]
        w3_hi_done = sem("w3_hi_done")
        w3_lo_done = sem("w3_lo_done")
        hid_hi_done = sem("hid_hi_done")
        hid_lo_done = sem("hid_lo_done")
        hid_done = sem("hid_done")
        summed = [sem(f"summed{n}") for n in range(4)]
        y_done = sem("y_done")
        yw_done = [sem(f"yw_done{s}") for s in range(2)]
        yw_free = [sem(f"yw_free{n}") for n in range(4)]
        scattered = [sem(f"scattered{n}") for n in range(4)]

        def cols(g):
            return slice(g * G_ROWS, g * G_ROWS + ROWS[g])

        WIDE = [(m, n) for m in range(2) for n in range(2)]

        def half(n):
            return slice(n * HALF, (n + 1) * HALF)

        S_BANK = ((0, 1), (2, 3))
        PT_BANK = 4
        PV_BANK, WO_BANK = 5, 6
        ROUTER_BANK = 7
        PLACE_BANK = 3

        block = ctx.enter_context(nc.Block())

        @block.sync
        def _(sp):
            for n in range(4):
                sp.sem_inc(summed[n], 1)
                sp.sem_inc(yw_free[n], 1)
            for s in range(2):
                sp.sem_inc(yw_done[s], 1)
            sp.sem_inc(hid_lo_done, 4)
            for g in range(GROUPS):
                sp.dma_start(x_sb[:, g, :, :], xT[g]).then_inc(in_x[g], 16)
                if g == 0:
                    sp.dma_start(pos[:, :], pos_cls).then_inc(in_pos, 16)
                    sp.dma_start(bias[:, :], bias_rows).then_inc(in_pos, 16)
            sp.dma_start(mask[:, :], c_mask).then_inc(in_attn, 16)
            sp.dma_start(bo_b[:, :], bo.partition_broadcast(G_ROWS)).then_inc(in_attn, 16)
            sp.dma_start(gate[:, :], betas.partition_broadcast(G_ROWS)).then_inc(in_attn, 16)
            sp.dma_start(z_sb[:, :, :], z4).then_inc(in_attn, 16)
            sp.dma_start(mem_bd[:, :, :], mem_diag).then_inc(in_attn, 16)
            sp.dma_start(head_rows[:, :, :], c_head).then_inc(in_attn, 16)
            for b in range(2):
                sp.dma_start(w12[b][:, :], w12T[b]).then_inc(w12_in[b], 16)
                sp.dma_start(w3[b][:, :], w3T[b]).then_inc(w3_in[b], 16)
                if b == 0:
                    sp.dma_start(gamma_b[:, :], gamma.partition_broadcast(G_ROWS)).then_inc(in_ffn, 16)
                    sp.dma_start(beta_b[:, :], beta.partition_broadcast(G_ROWS)).then_inc(in_ffn, 16)
                    sp.dma_start(router_sb[:, :, :], routerT).then_inc(in_ffn, 16)
                    sp.dma_start(before[:, :], c_before).then_inc(in_ffn, 16)
                    sp.dma_start(slot_iota[:, :], c_slots.partition_broadcast(G_ROWS)).then_inc(in_ffn, 16)
                    sp.dma_start(expert_iota[:, :], c_slots[0:EXPERTS].partition_broadcast(G_ROWS)).then_inc(in_ffn, 16)
                    sp.dma_start(token_plus1[:, :], c_token).then_inc(in_ffn, 16)
                    sp.dma_start(dup_far[:, :], c_dup).then_inc(in_ffn, 16)
            for g in range(GROUPS):
                sp.wait_ge(h2_done, g + 1)
                sp.dma_start(out[g * G_ROWS:g * G_ROWS + ROWS[g], :], h2[0:ROWS[g], g, :]).then_inc(h2_stored, 16)
            with sp.Fori(1, PAIRS) as i:
                for b in range(2):
                    sp.wait_ge(w12_lo_done[0], 4 * i + 2 * (b + 1) - 4)
                    sp.wait_ge(w12_lo_done[1], 4 * i + 2 * (b + 1) - 4)
                    sp.dma_start(w12[b][:, :], w12T[bass.ds(2 * i + b, 1)].rearrange("o p n -> (o p) n")).then_inc(w12_in[b], 16)
                    sp.wait_ge(w3_lo_done, 2 * i + b + 1 - 2)
                    sp.dma_start(w3[b][:, :], w3T[bass.ds(2 * i + b, 1)].rearrange("o p n -> (o p) n")).then_inc(w3_in[b], 16)
            for n in range(4):
                sp.wait_ge(scattered[n], 16 * PAIRS)
            sp.wait_ge(h2_stored, 16 * GROUPS)

        @block.tensor
        def _(pe):
            E_BANK, T_BANK, V_BANK = (0, 1), (2, 3), (4, 5)

            def embed(g):
                R = ROWS[g]
                if g == 0:
                    pe.wait_ge(in_embed, 16)
                if g >= 2:
                    pe.wait_ge(h_copied, g - 1)
                o = bank[E_BANK[g % 2]][0:R, 0:D]
                pe.wait_ge(in_x[g], 16)
                for k in range(KE):
                    mm = pe.matmul(o, x_sb[:, g, k, 0:R], wp_sb[:, k, :], start=(k == 0), stop=(k == KE - 1))
                mm.then_inc(embed_done, 1)

            def turn_hn(g):
                R = ROWS[g]
                if g == 0:
                    pe.wait_ge(in_ident, 16)
                pe.wait_ge(hn_done, g + 1)
                if g >= 2:
                    pe.wait_ge(hnT_done, g - 1)
                for k in range(KD):
                    tr = pe.transpose(bank[T_BANK[g % 2]][:, k * P:k * P + R], hn[0:R, g, k * P:(k + 1) * P], ident[0:R, 0:R])
                tr.then_inc(hnT_in_psum, 1)

            def value(g):
                R = ROWS[g]
                pe.wait_ge(hnT_done, g + 1)
                if g == 0:
                    pe.wait_ge(in_attn, 112)
                if g >= 2:
                    pe.wait_ge(v_done, g - 1)
                for k in range(KD):
                    mm = pe.matmul(bank[V_BANK[g % 2]][0:R, 0:D], hnT[:, k, cols(g)], w_sb[:, 2, k, :],
                                   start=(k == 0), stop=(k == KD - 1))
                mm.then_inc(v_in_psum, 1)

            for t in range(GROUPS + 2):
                if t < GROUPS:
                    embed(t)
                if 1 <= t <= GROUPS:
                    turn_hn(t - 1)
                if t >= 2:
                    value(t - 2)

            QK_BANK = (0, 1, 6, 7)
            pe.wait_ge(h_copied, GROUPS)
            for which in range(2):
                for n, (m, hf) in enumerate(WIDE):
                    if which == 1:
                        pe.wait_ge(q_done, n + 1)
                    for k in range(KD):
                        mm = pe.matmul(bank[QK_BANK[n]][:, 0:HALF], w_sb[:, which, k, m * P:(m + 1) * P],
                                       hnT[:, k, half(hf)], start=(k == 0), stop=(k == KD - 1))
                    mm.then_inc(qk_in_psum, 1)

            def memory_den():
                pe.wait_ge(v_done, GROUPS)
                for g in range(GROUPS):
                    R = ROWS[g]
                    for m in range(2):
                        if g == 0 or cols(g - 1).stop <= HALF < cols(g).stop:
                            pe.wait_ge(sq_done, (1 if g == 0 else 2) + 2 * m)
                        mm = pe.matmul(bank[4][0:R, g * HEADS:(g + 1) * HEADS], sqT[:, m, cols(g)], z_sb[:, m, :],
                                       start=(m == 0), stop=(m == 1))
                mm.then_inc(den_in_psum, 1)

            def memory_turn():
                pe.wait_ge(den_done, 1)
                for g in range(GROUPS):
                    R = ROWS[g]
                    b, c = g // (GROUPS // 2), g % (GROUPS // 2) * G_ROWS
                    tr = pe.transpose(bank[4 + b][0:2 * HEADS, c:c + R],
                                      den_split[0:R, g, :, :].bitcast(F32).rearrange("p s h -> p (s h)"), ident[0:R, 0:R])
                tr.then_inc(denT_in_psum, 1)

            def memory():
                pe.wait_ge(denT_done, 2)
                for n, (m, hf) in enumerate(WIDE):
                    if n == 0:
                        pe.wait_ge(k_done, 4)
                    if n >= 2:
                        pe.wait_ge(mem_done, n - 1)
                    pe.matmul(bank[4 + n % 2][:, 0:HALF], head_rows_r[:, m, :], denT[:, half(hf)], start=True, stop=True)
                    pe.matmul(bank[6 + n % 2][:, 0:HALF], mem_bd[:, m, :], sqT[:, m, half(hf)],
                              start=True, stop=True).then_inc(mem_in_psum, 1)

            def score(g):
                R = ROWS[g]
                if g >= 2:
                    pe.wait_ge(exp_done, g - 1)
                for hh in range(2):
                    pe.matmul(bank[S_BANK[g % 2][hh]][0:R, 0:2 * R].rearrange("p (h c) -> p h c", h=2), ident_bf[:, 0:R],
                              mask_bf[:, 0:R].unsqueeze(1).broadcast_to([G_ROWS, 2, R]), start=True, stop=False, skip_group_check=True)
                for hd in range(HEADS):
                    rows = slice(HD * (hd % 2), HD * (hd % 2) + HD)
                    mm = pe.matmul(bank[S_BANK[g % 2][hd % 2]][0:R, (hd // 2) * R:(hd // 2 + 1) * R], qT[rows, hd // 2, cols(g)],
                                   kT[rows, hd // 2, cols(g)], start=False, stop=True, skip_group_check=True)
                mm.then_inc(s_in_psum, 1)

            def turn_probs(g):
                R = ROWS[g]
                pe.wait_ge(pn_done, g + 1)
                if g == 0:
                    pe.wait_ge(mem_done, 4)
                if g >= 1:
                    pe.wait_ge(pT_done, g)
                for hd in range(HEADS):
                    tr = pe.transpose(bank[PT_BANK][0:R, hd * R:(hd + 1) * R], probs[0:R, g % 2, hd, 0:R], ident[0:R, 0:R])
                tr.then_inc(pT_in_psum, 1)

            def attend(g):
                R = ROWS[g]
                pe.wait_ge(pT_done, g + 1)
                if g >= 1:
                    pe.wait_ge(ao_done, g)
                for hd in range(HEADS):
                    rows = slice(HD * (hd % 2), HD * (hd % 2) + HD)
                    mm = pe.matmul(bank[PV_BANK][rows, (hd // 2) * R:(hd // 2 + 1) * R],
                                   v_sb[0:R, g, hd * HD:(hd + 1) * HD], probsT[0:R, g % 2, hd, 0:R], start=True, stop=True)
                mm.then_inc(pv_done, 1)

            def project(g):
                R = ROWS[g]
                pe.wait_ge(ao_done, g + 1)
                if g >= 1:
                    pe.wait_ge(h2_done, g)
                for k in range(2):
                    mm = pe.matmul(bank[WO_BANK][0:R, 0:D], aoT[:, g % 2, k, 0:R], w_sb[:, 3, k, :],
                                   start=(k == 0), stop=(k == 1))
                mm.then_inc(wo_done, 1)

            def turn_xn(g):
                R = ROWS[g]
                pe.wait_ge(xn_done, g + 1)
                if g >= 1:
                    pe.wait_ge(logits_read, g)
                for k in range(KD):
                    tr = pe.transpose(bank[ROUTER_BANK][:, k * P:k * P + R], xn[0:R, g, k * P:(k + 1) * P], ident[0:R, 0:R])
                tr.then_inc(xnT_in_psum, 1)

            def route(g):
                R = ROWS[g]
                pe.wait_ge(xnT_done, g + 1)
                for k in range(KD):
                    mm = pe.matmul(bank[ROUTER_BANK][0:R, 2 * P:2 * P + EXPERTS], xnT[:, g % 2, k, 0:R],
                                   router_sb[:, k, :], start=(k == 0), stop=(k == KD - 1))
                mm.then_inc(logits_in_psum, 1)

            memory_den()
            pe.wait_ge(k_done, 4)
            pe.wait_ge(mask_set, 1)
            score(0)
            score(1)
            memory_turn()
            memory()
            for t in range(GROUPS + 7):
                for lag, stage in ((6, route), (3, turn_probs), (4, project), (5, turn_xn), (0, score), (3, attend)):
                    if 0 <= t - lag < GROUPS and not (stage == score and t - lag < 2):
                        stage(t - lag)

            pe.wait_ge(hot_done, 1)
            for g in range(GROUPS - 1):
                later = GROUPS - 1 - g
                pe.matmul(bank[PLACE_BANK][0:G_ROWS, (g + 1) * EXPERTS:GROUPS * EXPERTS].rearrange("p (g e) -> p g e", e=EXPERTS),
                          ones[:, :], hot[:, g:g + 1, :].broadcast_to([G_ROWS, later, EXPERTS]),
                          start=(g == 0), stop=False, skip_group_check=True)
            pe.wait_ge(hot_done, 2)
            mm = pe.matmul(bank[PLACE_BANK][0:G_ROWS, 0:GROUPS * EXPERTS], before[:, :],
                           hot[:, :, :].rearrange("p g e -> p (g e)"), start=False, stop=True, skip_group_check=True)
            mm.then_inc(count_done, 1)

            def gather(i, b):
                pe.wait_ge(pick_done, 2 * (2 * i + b) + 1)
                for k in range(KD):
                    for part, x in enumerate((xn_hi, xn_lo)):
                        for g in range(GROUPS):
                            if k == 0 and part == 0 and g == GROUPS // 2:
                                pe.wait_ge(pick_done, 2 * (2 * i + b) + 2)
                            R = ROWS[g]
                            mm = pe.matmul(bank[4 + k][:, part * CW:(part + 1) * CW], x[0:R, g, k * P:(k + 1) * P],
                                           pick[0:R, g, :], start=(g == 0), stop=(g == GROUPS - 1))
                    mm.then_inc(gather_done, 1)

            def slot_info(i, b):
                for s in range(2):
                    o = bank[5][:, 2 * CW + 4 * s:2 * CW + 4 * s + 4]
                    for g in range(GROUPS):
                        R = ROWS[g]
                        mm = pe.matmul(o, pick[0:R, g, s * TAIL:s * TAIL + P],
                                       info[0:R, bass.ds(2 * i + b, 1), g, :].rearrange("p o c -> p (o c)"),
                                       start=(g == 0), stop=(g == GROUPS - 1))
                mm.then_inc(slots_in_psum, 1)

            def weights_ready(i, b):
                pe.wait_ge(w12_hi_done, W12_PARTS * (2 * i + b + 1))
                for n in range(2):
                    pe.wait_ge(w12_lo_done[n], W12_PARTS // 2 * (2 * i + b + 1))

            def gate_up(i, b, fc):
                hi, lo = (w.rearrange("p (k f) -> p k f", k=KD) for w in (w_split[b][0][:, :], w_split[b][1][:, :]))
                for part in range(2):
                    n = 2 * (fc % 2) + part
                    pe.wait_ge(summed[n], 4 * (2 * i + b) + fc // 2 + 1)
                    ws = slice(part * F + fc * P, part * F + (fc + 1) * P)
                    both, o = bank[n][:, 0:2 * CW], bank[n][:, 0:CW]
                    for k in range(KD):
                        tokens = xb[:, k, :, :].rearrange("p s c -> p (s c)")
                        if k < KD - 1:
                            pe.matmul(both, hi[:, k, ws], tokens, start=(k == 0), stop=False, skip_group_check=True)
                            pe.matmul(o, lo[:, k, ws], xb[:, k, 0, :], start=False, stop=False, skip_group_check=True)
                        else:
                            pe.matmul(o, lo[:, k, ws], xb[:, k, 0, :], start=False, stop=False, skip_group_check=True)
                            mm = pe.matmul(both, hi[:, k, ws], tokens, start=False, stop=True, skip_group_check=True)
                    mm.then_inc(gu_done, 1)

            def down(e, b, fc):
                hi, lo = (w.rearrange("p (f d) -> p f d", f=FC) for w in (w_split[b][2][:, :], w_split[b][3][:, :]))
                if fc == 0:
                    pe.wait_ge(w3_hi_done, e + 1)
                    pe.wait_ge(w3_lo_done, e + 1)
                    for s in range(2):
                        pe.wait_ge(yw_done[s], e + 1)
                pe.wait_ge(hid_hi_done, FC * e + fc + 1)
                pe.wait_ge(hid_lo_done, 4 + FC * e + fc + 1)
                for s in range(2):
                    o = bank[6 + s][:, 0:D]
                    slots = slice(s * TAIL, s * TAIL + P)
                    pe.matmul(o, hid_hi[b][:, fc, slots], hi[:, fc, :], start=(fc == 0), stop=False)
                    pe.matmul(o, hid_hi[b][:, fc, slots], lo[:, fc, :], start=False, stop=False)
                    mm = pe.matmul(o, hid_lo[b][:, fc, slots], hi[:, fc, :], start=False, stop=(fc == FC - 1))
                    if fc == FC - 1:
                        mm.then_inc(y_done, 1)

            def expert(i, b, first=False, last=False):
                pe.wait_ge(xb_done, 2 * (2 * i + b) + 2)
                slot_info(i, b)
                weights_ready(i, b)
                for fc in range(FC):
                    gate_up(i, b, fc)
                    if not first and fc % 2 == 1:
                        down(2 * i + b - 1, 1 - b, fc // 2)
                if not last:
                    gather(i + b, 1 - b)
                if not first:
                    for fc in range(FC // 2, FC):
                        down(2 * i + b - 1, 1 - b, fc)

            pe.wait_ge(xn_hi_done, GROUPS)
            pe.wait_ge(xn_lo_done, GROUPS)
            gather(0, 0)
            pe.wait_ge(info_done, 1)
            expert(0, 0, first=True)
            with pe.Fori(0, PAIRS - 1) as i:
                expert(i, 1)
                expert(i + 1, 0)
            expert(PAIRS - 1, 1, last=True)
            for fc in range(FC):
                down(EXPERTS - 1, 1, fc)

        @block.scalar
        def _(act):
            act.dma_start(wp_sb[:, :, :], wpT).then_inc(in_embed, 16)
            act.dma_start(ident[:, :], c_ident).then_inc(in_ident, 16)
            act.dma_start(w_sb[:, :, :, :], wqkvoT).then_inc(in_attn, 16)

            def copy_hnT(g):
                R = ROWS[g]
                act.wait_ge(hnT_in_psum, g + 1)
                act.activation(hnT[:, :, cols(g)], bank[2 + g % 2][:, 0:2 * P].rearrange("p (k c) -> p k c", k=KD)[:, :, 0:R],
                               ACT.Copy).then_inc(hnT_done, 1)

            def copy_v(g):
                R = ROWS[g]
                act.wait_ge(v_in_psum, g + 1)
                act.activation(v_sb[0:R, g, :], bank[4 + g % 2][0:R, 0:D], ACT.Copy).then_inc(v_done, 1)

            for t in range(GROUPS + 2):
                if 1 <= t <= GROUPS:
                    copy_hnT(t - 1)
                if t >= 2:
                    copy_v(t - 2)

            act.wait_ge(in_attn, 112)
            act.activation(gate[:, :], gate[:, :], ACT.Exp, scale=-1.0).then_inc(gate_exp, 1)
            QK_BANK = (0, 1, 6, 7)
            for n, (m, hf) in enumerate(WIDE):
                act.wait_ge(qk_in_psum, n + 1)
                act.activation(qT[:, m, half(hf)], bank[QK_BANK[n]][:, 0:HALF], ACT.Copy).then_inc(q_done, 1)
                act.wait_ge(qneg_done, n + 1)
                act.activation(qneg[:, m, half(hf)], qneg[:, m, half(hf)], ACT.Exp).then_inc(qexp_done, 1)
            for n, (m, hf) in enumerate(WIDE):
                act.wait_ge(qk_in_psum, 4 + n + 1)
                act.activation(kT[:, m, half(hf)], bank[QK_BANK[n]][:, 0:HALF], ACT.Copy).then_inc(k_done, 1)

            def split_w12(i, b, parts):
                for n in parts:
                    if n == 0:
                        act.wait_ge(w12_in[b], 16 * i + 16)
                    piece = slice(n * W12_PART, (n + 1) * W12_PART)
                    act.activation(w_split[b][0][:, piece], w12[b][:, piece], ACT.Copy).then_inc(w12_hi_done, 1)

            def softmax(t):
                R = ROWS[t]
                act.wait_ge(max_done, t + 1)
                if t >= 2:
                    act.wait_ge(pT_in_psum, t - 1)
                for hd in range(HEADS):
                    a = act.activation(probs[0:R, t % 2, hd, 0:R], bank[S_BANK[t % 2][hd % 2]][0:R, (hd // 2) * R:(hd // 2 + 1) * R], ACT.Exp,
                                       bias=negmax[0:R, t, hd:hd + 1], accum_out=psums[0:R, t, hd:hd + 1])
                a.then_inc(exp_done, 1)

            def copy_probsT(g):
                R = ROWS[g]
                act.wait_ge(pT_in_psum, g + 1)
                if g >= 2:
                    act.wait_ge(pv_done, g - 1)
                act.activation(probsT[0:R, g % 2, :, 0:R], bank[PT_BANK][0:R, 0:HEADS * R].rearrange("p (h c) -> p h c", h=HEADS),
                               ACT.Copy).then_inc(pT_done, 1)

            def split_xn(g):
                R = ROWS[g]
                act.wait_ge(xn_done, g + 1)
                act.activation(xn_hi[0:R, g, :], xn[0:R, g, :], ACT.Copy).then_inc(xn_hi_done, 1)

            def copy_xnT(g):
                R = ROWS[g]
                act.wait_ge(xnT_in_psum, g + 1)
                if g >= 2:
                    act.wait_ge(logits_in_psum, g - 1)
                act.activation(xnT[:, g % 2, :, 0:R], bank[ROUTER_BANK][:, 0:2 * P].rearrange("p (k c) -> p k c", k=KD)[:, :, 0:R],
                               ACT.Copy).then_inc(xnT_done, 1)

            split_w12(0, 0, (0, 1))
            softmax(0)
            act.wait_ge(denT_in_psum, 1)
            first = GROUPS // 2 * G_ROWS
            act.activation(denT[:, 0:first], bank[4][0:2 * HEADS, 0:first], ACT.Copy).then_inc(denT_done, 1)
            act.activation(denT[:, first:T], bank[5][0:2 * HEADS, 0:T - first], ACT.Copy).then_inc(denT_done, 1)
            for n in range(len(WIDE)):
                act.wait_ge(mem_in_psum, n + 1)
                if n >= 2:
                    act.wait_ge(mem_done, n - 1)
                act.activation(memgate[:, n % 2, :], bank[4 + n % 2][:, 0:HALF], ACT.Copy).then_inc(memgate_done, 1)
            for t in range(GROUPS + 7):
                for lag, stage in ((6, split_xn), (1, softmax), (5, copy_xnT), (2, copy_probsT)):
                    if 0 <= t - lag < GROUPS and not (stage == softmax and t - lag < 1):
                        stage(t - lag)
                if t in (2, 3):
                    split_w12(0, 0, (t,))
            act.wait_ge(gap_done, 1)
            act.activation(e1[:, :], gap[:, :], ACT.Exp).then_inc(e1_done, 1)

            W12_STEPS = (0, 2, 4, 6)

            def take_tokens(i, b):
                for k in range(KD):
                    act.wait_ge(gather_done, 2 * (2 * i + b) + k + 1)
                    act.activation(xb[:, k, :, :], bank[4 + k][:, 0:2 * CW].rearrange("p (b c) -> p b c", b=2),
                                   ACT.Copy).then_inc(xb_done, 1)

            def outputs(i, b):
                act.wait_ge(slots_done, 2 * i + b + 1)
                for s in range(2):
                    act.wait_ge(y_done, 2 * (2 * i + b) + s + 1)
                    act.wait_ge(yw_free[2 * b + s], i + 1)
                    act.activation(yw[2 * b + s], bank[6 + s][:, 0:D], ACT.Copy,
                                   scale=w_slot[b][:, s:s + 1]).then_inc(yw_done[s], 1)

            def expert(i, b, first=False, last=False):
                for fc in range(FC + 3):
                    if fc < FC:
                        for part in range(2):
                            n = 2 * (fc % 2) + part
                            act.wait_ge(gu_done, 2 * FC * (2 * i + b) + 2 * fc + part + 1)
                            act.wait_ge(summed[2 * ((fc - 1) % 2) + part], 4 * (2 * i + b) + (fc - 1) // 2 + 2)
                            act.activation(hi_lo[:, part, :], bank[n][:, CW:2 * CW], ACT.Copy).then_inc(hi_lo_out, 1)
                    if fc >= 3:
                        n = fc - 3
                        act.wait_ge(hid_done, FC * (2 * i + b) + n + 1)
                        act.activation(hid_hi[b][:, n, :], hid[:, n % 4, :], ACT.Copy).then_inc(hid_hi_done, 1)
                    if 1 <= fc <= FC:
                        n = fc - 1
                        act.wait_ge(summed[2 * (n % 2)], 4 * (2 * i + b) + n // 2 + 2)
                        act.activation(sg[:, n % 2, :], gate_sum[:, n % 2, :], ACT.Silu).then_inc(silu_done, 1)
                    if not last and fc in W12_STEPS:
                        split_w12(i + b, 1 - b, (W12_STEPS.index(fc),))
                    if not last and fc == FC:
                        take_tokens(i + b, 1 - b)
                if not first:
                    outputs(i + b - 1, 1 - b)

            act.wait_ge(h2_stored, 16 * GROUPS)
            take_tokens(0, 0)
            expert(0, 0, first=True)
            with act.Fori(0, PAIRS - 1) as i:
                expert(i, 1)
                expert(i + 1, 0)
            expert(PAIRS - 1, 1, last=True)
            outputs(PAIRS - 1, 1)

        @block.vector
        def _(dve):
            steps = [0]

            def then(ins):
                steps[0] += 1
                ins.then_inc(dve_step, 1)
                dve.wait_ge(dve_step, steps[0])

            dve.memset(minus_half[:, :], -0.5).then_inc(consts_set, 1)
            dve.memset(ones[:, :], 1.0)
            dve.wait_ge(in_ident, 16)
            dve.tensor_copy(ident_bf[:, :], ident[0:G_ROWS, 0:G_ROWS])
            dve.memset(logits[:, :, :], 0.0)
            dve.memset(top[:, :, :], 0.0)
            dve.memset(top_i[:, :, :], 0)
            dve.memset(den[:, :, :], 1.0)
            dve.memset(hot[:, :, :], 0.0)
            then(dve.memset(info[:, :, :, :].bitcast(F32), 0.0))

            def norm1(g):
                R = ROWS[g]
                dve.wait_ge(rstd1_done, g + 1)
                dve.tensor_scalar(hn[0:R, g, :], h[0:R, g, :], mv1[0:R, g, 0:1], rstd1[0:R, g:g + 1],
                                  ALU.subtract, ALU.mult).then_inc(hn_done, 1)

            for g in range(GROUPS):
                R = ROWS[g]
                dve.wait_ge(embed_done, g + 1)
                if g == 0:
                    dve.wait_ge(pos_done, 1)
                dve.tensor_tensor(h[0:R, g, :], bank[g % 2][0:R, 0:D], pos[0:R, :], ALU.add).then_inc(h_copied, 1)
                dve.wait_ge(h_copied, g + 1)
                then(dve.bn_stats(stats[0:R, g, :], h[0:R, g, :]))
                then(dve.bn_aggr(mv1[0:R, g, :], stats[0:R, g, :]))
                dve.tensor_scalar(var1[0:R, g:g + 1], mv1[0:R, g, 1:2], EPS, None, ALU.add).then_inc(var1_done, 1)
                norm1(g)

            dve.wait_ge(in_attn, 112)
            dve.tensor_copy(head_rows_r[:, :, :], head_rows[:, :, :])
            dve.tensor_copy(mask_bf[:, :], mask[:, :]).then_inc(mask_set, 1)
            dve.wait_ge(gate_exp, 1)
            then(dve.tensor_scalar(gate[:, :], gate[:, :], 1.0, None, ALU.add))
            then(dve.reciprocal(gate[:, :], gate[:, :]))
            then(dve.tensor_scalar(keep[:, :], gate[:, :], -1.0, 1.0, ALU.mult, ALU.add))

            for n, (m, hf) in enumerate(WIDE):
                dve.wait_ge(q_done, n + 1)
                dve.tensor_scalar(qneg[:, m, half(hf)], qT[:, m, half(hf)], 0.0, None, ALU.min).then_inc(qneg_done, 1)
            for n, (m, hf) in enumerate(WIDE):
                dve.wait_ge(qexp_done, n + 1)
                dve.scalar_tensor_tensor(out=sqT[:, m, half(hf)], in0=qT[:, m, half(hf)], scalar=0.0,
                                         in1=qneg[:, m, half(hf)], op0=ALU.max, op1=ALU.add).then_inc(sq_done, 1)

            def row_max(g):
                R = ROWS[g]
                dve.wait_ge(s_in_psum, g + 1)
                for hh in range(2):
                    max_ins = dve.tensor_reduce(negmax[0:R, g, hh::2], bank[S_BANK[g % 2][hh]][0:R, 0:2 * R].rearrange("p (h c) -> p h c", h=2),
                                                AX_X, ALU.max)
                then(max_ins)
                dve.tensor_scalar(negmax[0:R, g, :], negmax[0:R, g, :], -1.0, None, ALU.mult).then_inc(max_done, 1)

            def memory_den():
                dve.wait_ge(den_in_psum, 1)
                full = (GROUPS - 1) * HEADS
                den2 = den[:, :, :].rearrange("p g h -> p (g h)")
                dve.tensor_scalar(den2[:, 0:full], bank[4][0:G_ROWS, 0:full], 1e-6, None, ALU.add)
                then(dve.tensor_scalar(den2[0:ROWS[-1], full:full + HEADS], bank[4][0:ROWS[-1], full:full + HEADS], 1e-6, None, ALU.add))
                then(dve.reciprocal(den2, den2))
                then(dve.tensor_tensor(den[:, :, :], den[:, :, :], gate[:, :].unsqueeze(1).broadcast_to([G_ROWS, GROUPS, HEADS]), ALU.mult))
                then(dve.tensor_copy(den_split[:, :, 0, :], den[:, :, :]))
                dve.tensor_tensor(den_split[:, :, 1, :], den[:, :, :], den_split[:, :, 0, :].bitcast(F32),
                                  ALU.subtract).then_inc(den_done, 1)

            def memory_part(n, m, hf):
                dve.wait_ge(memgate_done, n + 1)
                dve.tensor_tensor(memT[:, m, half(hf)], bank[6 + n % 2][:, 0:HALF], memgate[:, n % 2, :], ALU.mult).then_inc(mem_done, 1)

            def normalise(g):
                R = ROWS[g]
                dve.wait_ge(exp_done, g + 1)
                then(dve.reciprocal(psums[0:R, g, :], psums[0:R, g, :]))
                then(dve.tensor_tensor(psums[0:R, g, :], psums[0:R, g, :], keep[0:R, :], ALU.mult))
                dve.tensor_tensor(probs[0:R, g % 2, :, 0:R], probs[0:R, g % 2, :, 0:R],
                                  psums[0:R, g, :].unsqueeze(2).broadcast_to([R, HEADS, R]), ALU.mult).then_inc(pn_done, 1)

            def add_memory(g):
                R = ROWS[g]
                dve.wait_ge(pv_done, g + 1)
                if g == 0:
                    dve.wait_ge(mem_done, 4)
                if g >= 2:
                    dve.wait_ge(wo_done, g - 1)
                dve.tensor_tensor(aoT[:, g % 2, :, 0:R], bank[PV_BANK][:, 0:2 * R].rearrange("p (m c) -> p m c", m=2),
                                  memT[:, :, cols(g)], ALU.add).then_inc(ao_done, 1)

            def residual(g):
                R = ROWS[g]
                dve.wait_ge(wo_done, g + 1)
                dve.wait_ge(h_bo_done, g + 1)
                dve.tensor_tensor(h2[0:R, g, :], bank[WO_BANK][0:R, 0:D], h[0:R, g, :], ALU.add).then_inc(h2_done, 1)
                dve.wait_ge(h2_done, g + 1)
                then(dve.bn_stats(stats[0:R, g, :], h2[0:R, g, :]))
                then(dve.bn_aggr(mv2[0:R, g, :], stats[0:R, g, :]))
                dve.tensor_scalar(var2[0:R, g:g + 1], mv2[0:R, g, 1:2], 1.0 + EPS, EPS * EPS, ALU.mult, ALU.add).then_inc(var2_done, 1)

            def norm2(g):
                R = ROWS[g]
                if g == 0:
                    dve.wait_ge(in_ffn, 128)
                then(dve.scalar_tensor_tensor(out=xg[0:R, g, :], in0=h2[0:R, g, :], scalar=mv2[0:R, g, 0:1],
                                              in1=gamma_b[0:R, :], op0=ALU.subtract, op1=ALU.mult))
                dve.wait_ge(rstd2_done, g + 1)
                dve.scalar_tensor_tensor(out=xn[0:R, g, :], in0=xg[0:R, g, :], scalar=rstd2[0:R, g:g + 1],
                                         in1=beta_b[0:R, :], op0=ALU.mult, op1=ALU.add).then_inc(xn_done, 1)

            def rank(g):
                R = ROWS[g]
                dve.wait_ge(logits_in_psum, g + 1)
                dve.tensor_scalar(logits[0:R, g, :], bank[ROUTER_BANK][0:R, 2 * P:2 * P + EXPERTS], 1e4, -1e4,
                                  ALU.min, ALU.max).then_inc(logits_read, 1)
                dve.wait_ge(logits_read, g + 1)
                then(dve.max(top[0:R, g, :], logits[0:R, g, :]))
                then(dve.max_index(top_i[0:R, g, :], top[0:R, g, :], logits[0:R, g, :]))

            def choices(g0, g1):
                R, gs = ROWS[g0], slice(g0, g1)
                then(dve.tensor_copy(top_f[:, gs, :], top_i[:, gs, :]))
                hots = expert_iota[:, :].unsqueeze(1).broadcast_to([G_ROWS, g1 - g0, EXPERTS])
                dve.tensor_tensor(hot0[:, gs, :], hots, top_f[:, gs, 0:1].broadcast_to([G_ROWS, g1 - g0, EXPERTS]), ALU.is_equal)
                then(dve.tensor_tensor(hot1[:, gs, :], hots, top_f[:, gs, 1:2].broadcast_to([G_ROWS, g1 - g0, EXPERTS]), ALU.is_equal))
                dve.tensor_tensor(hot[0:R, gs, :], hot0[0:R, gs, :], hot1[0:R, gs, :], ALU.add).then_inc(hot_done, 1)

            def split_w12(i, b):
                for n in range(W12_PARTS // 2, W12_PARTS):
                    dve.wait_ge(w12_hi_done, W12_PARTS * (2 * i + b) + n + 1)
                    piece = slice(n * W12_PART, (n + 1) * W12_PART)
                    yield dve.tensor_tensor(w_split[b][1][:, piece], w12[b][:, piece], w_split[b][0][:, piece].bitcast(F32),
                                            ALU.subtract).then_inc(w12_lo_done[0], 1)

            def split_w3(i, b):
                dve.wait_ge(w3_in[b], 16 * i + 16)
                dve.tensor_copy(w_split[b][2][:, :], w3[b][:, :]).then_inc(w3_hi_done, 1)

            def choose(i, b, halves=(0, 1)):
                for part in halves:
                    gs = (slice(0, GROUPS // 2), slice(GROUPS // 2, GROUPS))[part]
                    n = gs.stop - gs.start
                    dve.tensor_tensor(pick[:, gs, :], slot_iota[:, :].unsqueeze(1).broadcast_to([G_ROWS, n, CW]),
                                      place[:, bass.ds(2 * i + b, 1), gs].rearrange("p o g -> p (o g)").unsqueeze(2).broadcast_to([G_ROWS, n, CW]),
                                      ALU.is_equal).then_inc(pick_done, 1)

            memory_den()
            row_max(0)
            row_max(1)
            for n, (m, hf) in enumerate(WIDE):
                memory_part(n, m, hf)
            first_w12 = split_w12(0, 0)
            for t in range(GROUPS + 7):
                for lag, stage in ((5, residual), (4, add_memory), (1, row_max), (6, rank), (5, norm2), (2, normalise)):
                    if 0 <= t - lag < GROUPS and not (stage == row_max and t - lag < 2):
                        stage(t - lag)
                if t in (3, 4):
                    next(first_w12)
                if t == GROUPS + 4:
                    choices(0, GROUPS - 1)
            choices(GROUPS - 1, GROUPS)
            dve.wait_ge(count_done, 1)
            place_gp = place[:, :, :].rearrange("p e g -> p g e")
            then(dve.scalar_tensor_tensor(out=place_gp, in0=bank[PLACE_BANK][0:G_ROWS, 0:GROUPS * EXPERTS].rearrange("p (g e) -> p g e", e=EXPERTS),
                                          scalar=1.0, in1=hot[:, :, :], op0=ALU.add, op1=ALU.mult))
            dve.tensor_scalar(place[:, :, :], place[:, :, :], -1.0, None, ALU.add).then_inc(place_done, 1)
            dve.wait_ge(place_done, 1)
            dve.wait_ge(xn_lo_done, GROUPS)
            choose(0, 0)
            dve.tensor_tensor(gap[:, :], top[:, :, 1], top[:, :, 0], ALU.subtract).then_inc(gap_done, 1)
            dve.wait_ge(e1_done, 1)
            then(dve.tensor_scalar(p0[:, :], e1[:, :], 1.0, 1e-12, ALU.add, ALU.add))
            then(dve.reciprocal(p0[:, :], p0[:, :]))
            then(dve.tensor_tensor(p1[:, :], p0[:, :], e1[:, :], ALU.mult))
            wt_gp = wt[:, :, :].rearrange("p e g -> p g e")
            wt1_gp = wt1[:, :, :].rearrange("p e g -> p g e")
            dve.tensor_tensor(wt_gp, hot0[:, :, :], p0[:, :].unsqueeze(2).broadcast_to([G_ROWS, GROUPS, EXPERTS]), ALU.mult)
            then(dve.tensor_tensor(wt1_gp, hot1[:, :, :], p1[:, :].unsqueeze(2).broadcast_to([G_ROWS, GROUPS, EXPERTS]), ALU.mult))
            then(dve.tensor_tensor(wt[:, :, :], wt[:, :, :], wt1[:, :, :], ALU.add))
            dve.tensor_copy(info[:, :, :, 0], token_plus1[:, :].unsqueeze(1).broadcast_to([G_ROWS, EXPERTS, GROUPS]))
            then(dve.tensor_copy(info[:, :, :, 1], wt[:, :, :]))
            dve.tensor_tensor(info[:, :, :, 2], wt[:, :, :], info[:, :, :, 1].bitcast(F32), ALU.subtract).then_inc(info_done, 1)

            def take_slots(i, b):
                dve.wait_ge(slots_in_psum, 2 * i + b + 1)
                dve.tensor_copy(slot_raw[:, :, :], bank[5][:, 2 * CW:2 * CW + 8].rearrange("p (n c) -> p n c", c=4)).then_inc(slots_stage, 1)

            def slots(i, b):
                step = 4 * (2 * i + b)
                dve.wait_ge(yw_free[2 * b + 1], i + 1)
                dve.wait_ge(slots_stage, step + 1)
                dve.tensor_tensor(w_slot[b][:, :], slot_raw[:, :, 1], slot_raw[:, :, 2], ALU.add)
                dve.tensor_scalar(slot_far[:, :], slot_raw[:, :, 0], 0.0, FAR, ALU.is_equal, ALU.mult).then_inc(slots_stage, 1)
                dve.wait_ge(slots_stage, step + 2)
                dve.scalar_tensor_tensor(out=slot_row[:, :], in0=slot_raw[:, :, 0], scalar=-1.0, in1=slot_far[:, :],
                                         op0=ALU.add, op1=ALU.add).then_inc(slots_stage, 1)
                dve.wait_ge(slots_stage, step + 3)
                dve.tensor_tensor(slot_row[:, :], slot_row[:, :], dup_far[:, :], ALU.add).then_inc(slots_stage, 1)
                dve.wait_ge(slots_stage, step + 4)
                dve.tensor_copy(slot_token[b][:, :], slot_row[:, :]).then_inc(slots_done, 1)

            def expert(i, b, first=False, last=False):
                pieces = None if last else split_w12(i + b, 1 - b)
                for fc in range(FC + 4):
                    if 2 <= fc <= FC + 1:
                        n = fc - 2
                        dve.wait_ge(hid_lo_done, FC * (2 * i + b) + n + 1)
                        dve.wait_ge(silu_done, FC * (2 * i + b) + n + 1)
                        dve.wait_ge(summed[2 * (n % 2) + 1], 4 * (2 * i + b) + n // 2 + 2)
                        dve.tensor_tensor(hid[:, n % 4, :], sg[:, n % 2, :], up_sum[:, n % 4, :], ALU.mult).then_inc(hid_done, 1)
                    if fc >= 4:
                        n = fc - 4
                        dve.wait_ge(hid_hi_done, FC * (2 * i + b) + n + 1)
                        dve.tensor_tensor(hid_lo[b][:, n, :], hid[:, n % 4, :], hid_hi[b][:, n, :].bitcast(F32),
                                          ALU.subtract).then_inc(hid_lo_done, 1)
                    if fc < FC:
                        for part, total in enumerate((gate_sum[:, fc % 2, :], up_sum[:, fc % 4, :])):
                            n = 2 * (fc % 2) + part
                            dve.wait_ge(hi_lo_out, 2 * FC * (2 * i + b) + 2 * fc + part + 1)
                            dve.tensor_tensor(total, bank[n][:, 0:CW], hi_lo[:, part, :], ALU.add).then_inc(summed[n], 1)
                    if fc == 1:
                        if not first:
                            dve.wait_ge(yw_done[1], 2 * i + b)
                        split_w3(i, b)
                    if fc == 0:
                        take_slots(i, b)
                    if fc == 6:
                        slots(i, b)
                    if not last:
                        if fc in (2, 3):
                            choose(i + b, 1 - b, (fc - 2,))
                        if fc in (FC, FC + 2):
                            next(pieces)

            expert(0, 0, first=True)
            with dve.Fori(0, PAIRS - 1) as i:
                expert(i, 1)
                expert(i + 1, 0)
            expert(PAIRS - 1, 1, last=True)

        @block.gpsimd
        def _(pool):
            pool.wait_ge(in_pos, 32)
            pool.tensor_tensor(pos[:, :], pos[:, :], bias[:, :], ALU.add).then_inc(pos_done, 1)
            pool.wait_ge(consts_set, 1)
            for g in range(GROUPS):
                R = ROWS[g]
                pool.wait_ge(var1_done, g + 1)
                pool.tensor_tensor(rstd1[0:R, g:g + 1], var1[0:R, g:g + 1], minus_half[0:R, :], ALU.pow).then_inc(rstd1_done, 1)
            pool.wait_ge(in_attn, 112)
            for g in range(GROUPS):
                R = ROWS[g]
                pool.wait_ge(hn_done, g + 1)
                pool.tensor_tensor(h[0:R, g, :], h[0:R, g, :], bo_b[0:R, :], ALU.add).then_inc(h_bo_done, 1)

            def split_w12(e, n):
                pool.wait_ge(w12_hi_done, W12_PARTS * e + n + 1)
                piece = slice(n * W12_PART, (n + 1) * W12_PART)
                pool.tensor_tensor(w_split[e % 2][1][:, piece], w12[e % 2][:, piece], w_split[e % 2][0][:, piece].bitcast(F32),
                                   ALU.subtract).then_inc(w12_lo_done[1], 1)

            def split_w3(e):
                pool.wait_ge(w3_hi_done, e + 1)
                pool.tensor_tensor(w_split[e % 2][3][:, :], w3[e % 2][:, :], w_split[e % 2][2][:, :].bitcast(F32),
                                   ALU.subtract).then_inc(w3_lo_done, 1)

            def split_xn(g):
                R = ROWS[g]
                pool.wait_ge(xn_hi_done, g + 1)
                pool.tensor_tensor(xn_lo[0:R, g, :], xn[0:R, g, :], xn_hi[0:R, g, :].bitcast(F32), ALU.subtract).then_inc(xn_lo_done, 1)

            for n in range(W12_PARTS // 2):
                split_w12(0, n)
            for t in range(GROUPS + 1):
                if t < GROUPS:
                    R = ROWS[t]
                    pool.wait_ge(var2_done, t + 1)
                    pool.tensor_tensor(rstd2[0:R, t:t + 1], var2[0:R, t:t + 1], minus_half[0:R, :], ALU.pow).then_inc(rstd2_done, 1)
                if t >= 1:
                    split_xn(t - 1)
            def scatter(e, s):
                n = 2 * (e % 2) + s
                pool.wait_ge(yw_done[s], e + 2)
                pool.indirect_dma_start(out=out, out_offset=bass.IndirectOffsetOnAxis(ap=slot_token[e % 2][:, s:s + 1], axis=0),
                                        in_=yw[n], in_offset=None, bounds_check=T - 1, oob_is_err=False,
                                        compute_op=ALU.add).then_inc(scattered[n], 16)

            def scatter_end(e, s):
                n = 2 * (e % 2) + s
                pool.wait_ge(scattered[n], 16 * (e // 2) + 16)
                pool.sem_inc(yw_free[n], 1)

            pool.wait_ge(h2_stored, 16 * GROUPS)
            for e in range(EXPERTS + 2):
                for s in range(2):
                    if e >= 2:
                        scatter(e - 2, s)
                    if e + 1 < EXPERTS:
                        split_w12(e + 1, s)
                    if e >= 2:
                        scatter_end(e - 2, s)
                if e < EXPERTS:
                    split_w3(e)


def _constants():
    q = np.arange(G_ROWS)
    seen = (q[:, None] // S == q[None, :] // S) & (q[:, None] >= q[None, :])
    mask = np.where(seen, 0, MASKED).astype(np.float32)
    before = (q[:, None] < q[None, :]).astype(np.float32)
    slots = np.arange(CW, dtype=np.float32)
    slots[CAP:] = -2 - np.arange(CW - CAP)
    token = np.minimum(q[:, None] + G_ROWS * np.arange(GROUPS)[None, :] + 1, T).astype(np.float32)
    dup = np.zeros((P, 2), np.float32)
    dup[:P - TAIL, 1] = FAR
    head = np.zeros((2, HEADS, 2, P), np.float32)
    for n in range(HEADS):
        head[:, n, n // 2, n % 2 * HD:(n % 2 + 1) * HD] = 1
    return [mask, before, np.eye(P, dtype=np.float32), slots, token, dup, head.reshape(2 * HEADS, 2, P)]


def kernel(x, cls_tok, L0_tok_W_proj, L0_tok_b_proj, L0_tok_pos_emb, L0_attn_Wq, L0_attn_Wk, L0_attn_Wv, L0_attn_Wo,
           L0_attn_bo, L0_attn_betas, L0_attn_mem, L0_attn_z, L0_ffn_ln_gamma, L0_ffn_ln_beta, L0_ffn_router_w,
           L0_ffn_w12, L0_ffn_w3):
    import concourse.bacc as bacc
    from concourse.bass_utils import run_bass_kernel_spmd

    side = SIDE // PATCH

    def to_partitions(a, k):
        return a.reshape(k, P, -1).transpose(1, 0, 2)

    patches = np.asarray(x).reshape(IMAGES, side, PATCH, side, PATCH, CHANNELS).transpose(0, 1, 3, 2, 4, 5).reshape(IMAGES, NPATCH, -1)
    tokens = np.pad(patches, ((0, 0), (1, 0), (0, 0))).reshape(T, -1)
    tokens = np.pad(tokens, ((0, GROUPS * G_ROWS - T), (0, 0))).reshape(GROUPS, G_ROWS, KE, P)
    image_rows = np.concatenate([np.asarray(cls_tok)[0], np.asarray(L0_tok_pos_emb)])
    bias_rows = np.zeros_like(image_rows)
    bias_rows[1:] = np.asarray(L0_tok_b_proj)
    mem, z = np.asarray(L0_attn_mem), np.asarray(L0_attn_z)
    mem_diag = np.zeros((P, 2, P), mem.dtype)
    z4 = np.zeros((P, 2, HEADS), z.dtype)
    for n in range(HEADS):
        rows = slice(n % 2 * HD, (n % 2 + 1) * HD)
        mem_diag[rows, n // 2, rows] = mem[n]
        z4[rows, n // 2, n] = z[n, :, 0]
    weights = [np.asarray(w).T for w in (L0_attn_Wq, L0_attn_Wk, L0_attn_Wv, L0_attn_Wo)]
    arrays = [
        tokens.transpose(0, 3, 2, 1),
        to_partitions(np.asarray(L0_tok_W_proj).T, KE),
        np.tile(image_rows, (IMG_PER_GROUP, 1)),
        np.tile(bias_rows, (IMG_PER_GROUP, 1)),
        np.stack([to_partitions(w, KD) for w in weights], axis=1),
        np.asarray(L0_attn_bo), np.asarray(L0_attn_betas).reshape(HEADS), mem_diag, z4,
        np.asarray(L0_ffn_ln_gamma), np.asarray(L0_ffn_ln_beta),
        to_partitions(np.asarray(L0_ffn_router_w).T, KD),
        np.asarray(L0_ffn_w12).transpose(0, 2, 1).reshape(EXPERTS, KD, P, 2 * F).transpose(0, 2, 1, 3).reshape(EXPERTS, P, -1),
        np.asarray(L0_ffn_w3).transpose(0, 2, 1).reshape(EXPERTS, FC, P, D).transpose(0, 2, 1, 3).reshape(EXPERTS, P, -1),
    ] + _constants()

    nc = bacc.Bacc("TRN2", target_bir_lowering=False, num_devices=1)
    inputs, args = {}, []
    for n, a in enumerate(arrays):
        a = np.ascontiguousarray(a)
        inputs[f"in{n}"] = a
        args.append(nc.dram_tensor(f"in{n}", a.shape, mybir.dt.from_np(a.dtype), kind="ExternalInput").ap())
    args.append(nc.dram_tensor("out", (T, D), F32, kind="ExternalOutput").ap())
    vit_tower(nc, *args)
    r = run_bass_kernel_spmd(nc, [inputs], core_ids=[0])
    return r.results[0]["out"].reshape(IMAGES, S, D)
```
